# Optimizing a Trainium2 kernel written in Bass

```python
import numpy as np
import jax
import jax.numpy as jnp

def _softmax(x, axis=-1):
    return jax.nn.softmax(x, axis=axis)

def _gelu(x):
    return jax.nn.gelu(x, approximate=True)

def _silu(x):
    return jax.nn.silu(x)

def _sigmoid(x):
    return jax.nn.sigmoid(x)

def _layernorm(x, axis=-1, eps=1e-05):
    m = jnp.mean(x, axis=axis, keepdims=True)
    v = jnp.var(x, axis=axis, keepdims=True)
    return (x - m) / jnp.sqrt(v + eps)

def _scatter_add(tgt, idx, src, axis=0):
    return tgt.at[idx].add(src)

def _segment_sum(src, seg, n):
    return jax.ops.segment_sum(src, seg, n)
kernel_name = 'mk_perceiver_d1_seqx_r4_fdb3e6'

def setup_inputs(seed: int=0):
    np.random.seed(seed)
    _w = jnp.asarray

    def _rec_inputs():
        import jax
        import jax.numpy as jnp
        _rk = jax.random.key(seed)
        x = -0.0003929 + 0.9999 * jax.random.normal(jax.random.fold_in(_rk, 1), (2, 64, 1024), jnp.float32)
        _lenS = 64 - jax.random.randint(jax.random.fold_in(_rk, 7), (2,), 0, max(1, 64 // 4) + 1, jnp.int32)
        _lenS2 = 1024 - jax.random.randint(jax.random.fold_in(_rk, 8), (2,), 0, max(1, 1024 // 4) + 1, jnp.int32)
        _ctx_4096P = jax.random.normal(jax.random.fold_in(_rk, 11), (2, 16, 1024), jnp.float32)
        _ctx_4096c = jax.random.dirichlet(jax.random.fold_in(_rk, 511), 0.3 * jnp.ones((16,), jnp.float32), (2, 1024))
        _ctx_4096t = jnp.einsum('bsk,bkd->bsd', _ctx_4096c, _ctx_4096P)
        _ctx_4096t = _ctx_4096t * jax.lax.rsqrt(jnp.mean(jnp.square(_ctx_4096t)) + 1e-12) * 0.953939
        ctx_4096 = 2.81802e-05 + 1.00001 * (_ctx_4096t + 0.3 * jax.random.normal(jax.random.fold_in(_rk, 611), (2, 1024, 1024), jnp.float32))
        _validS = jnp.arange(64)[None, :] < _lenS[:, None]
        _validS2 = jnp.arange(1024)[None, :] < _lenS2[:, None]
        _causal = jnp.tril(jnp.ones((64, 64), dtype=bool))
        mask_BxSxS2_ff0 = jnp.where(jnp.ones((2, 64, 1024), dtype=bool), 0.0, -1000000000.0).astype(jnp.float32)
        return (x, ctx_4096, mask_BxSxS2_ff0)
    x, ctx_4096, mask_BxSxS2_ff0 = _rec_inputs()

    def _L0_xattn_setup():
        import jax, jax.numpy as jnp
        import numpy as np
        BS, SEQ, D_MODEL = (4, 256, 1024)
        N_Q_HEADS, N_KV_HEADS, D_K, D_V = (32, 8, 128, 128)
        ROPE_BASE = 10000.0

        def _rotate_half(x):
            x1, x2 = jnp.split(x, 2, axis=-1)
            return jnp.concatenate([-x2, x1], axis=-1)

        def _apply_rope(x, pos0):
            d = x.shape[-1]
            seq = x.shape[2]
            inv_freq = 1.0 / ROPE_BASE ** (jnp.arange(0, d, 2, dtype=jnp.float32) / d)
            pos = (pos0 + jnp.arange(seq)).astype(jnp.float32)
            ang = pos[:, None] * inv_freq[None, :]
            cos = jnp.concatenate([jnp.cos(ang), jnp.cos(ang)], axis=-1)
            sin = jnp.concatenate([jnp.sin(ang), jnp.sin(ang)], axis=-1)
            return x * cos[None, None] + _rotate_half(x) * sin[None, None]
        key = jax.random.key(seed)
        ks = jax.random.split(key, 8)
        w_scale = 0.02
        return {'query': jax.random.normal(ks[0], (BS, SEQ, D_MODEL), dtype=jnp.float32), 'key': jax.random.normal(ks[1], (BS, SEQ, D_MODEL), dtype=jnp.float32), 'value': jax.random.normal(ks[2], (BS, SEQ, D_MODEL), dtype=jnp.float32), 'mask': jnp.zeros((BS, SEQ, SEQ), dtype=jnp.float32), 'wq': jax.random.normal(ks[3], (D_MODEL, N_Q_HEADS * D_K), dtype=jnp.float32) * w_scale, 'wk': jax.random.normal(ks[4], (D_MODEL, N_KV_HEADS * D_K), dtype=jnp.float32) * w_scale, 'wv': jax.random.normal(ks[5], (D_MODEL, N_KV_HEADS * D_V), dtype=jnp.float32) * w_scale, 'wo': jax.random.normal(ks[6], (N_Q_HEADS * D_V, D_MODEL), dtype=jnp.float32) * w_scale, 'curr_seq_pos': 0}
    _L0_xattn_all = _L0_xattn_setup()
    _L0_xattn_in = {k: v for k, v in _L0_xattn_all.items() if k in ('wq', 'wk', 'wv', 'wo')}
    del _L0_xattn_all

    def _L0_attn_setup():
        import jax, jax.numpy as jnp
        import numpy as np
        import math
        FACTOR = 1
        key = jax.random.key(seed)
        x = jax.random.normal(key, (8, 128, 1024), dtype=jnp.float32)
        return {'x': x}
    _L0_attn_all = _L0_attn_setup()
    _L0_attn_in = {k: v for k, v in _L0_attn_all.items() if k in ()}
    del _L0_attn_all

    def _L0_ffn_setup():
        import jax, jax.numpy as jnp
        import numpy as np
        LORA_R = 16
        SCALE = 16.0 / np.sqrt(16.0)
        NUM_EXPERTS = 4
        TOP_K = 2
        IN_F = 1024
        OUT_F = 1024
        key = jax.random.key(seed)
        k_x, k_a, k_b, k_r = jax.random.split(key, 4)
        x = jax.random.normal(k_x, (2, 512, IN_F), dtype=jnp.float32)
        A = jax.random.normal(k_a, (NUM_EXPERTS, LORA_R, IN_F), dtype=jnp.float32) * (1.0 / np.sqrt(IN_F))
        B = jax.random.normal(k_b, (NUM_EXPERTS, OUT_F, LORA_R), dtype=jnp.float32) * 0.02
        Wr = jax.random.normal(k_r, (NUM_EXPERTS, IN_F), dtype=jnp.float32) * 0.02
        return {'x': x, 'A': A, 'B': B, 'Wr': Wr}
    _L0_ffn_all = _L0_ffn_setup()
    _L0_ffn_in = {k: v for k, v in _L0_ffn_all.items() if k in ('A', 'B', 'Wr')}
    del _L0_ffn_all
    return {'x': x, 'ctx_4096': ctx_4096, 'mask_BxSxS2_ff0': mask_BxSxS2_ff0, 'L0_xattn_wq': _L0_xattn_in['wq'], 'L0_xattn_wk': _L0_xattn_in['wk'], 'L0_xattn_wv': _L0_xattn_in['wv'], 'L0_xattn_wo': _L0_xattn_in['wo'], 'L0_ffn_A': _L0_ffn_in['A'], 'L0_ffn_B': _L0_ffn_in['B'], 'L0_ffn_Wr': _L0_ffn_in['Wr']}

def reference(x, ctx_4096, mask_BxSxS2_ff0, L0_xattn_wq, L0_xattn_wk, L0_xattn_wv, L0_xattn_wo, L0_ffn_A, L0_ffn_B, L0_ffn_Wr):
    import jax
    import jax.numpy as jnp

    def _L0_xattn_ref(query, key, value, mask, wq, wk, wv, wo, curr_seq_pos):
        import jax, jax.numpy as jnp
        import numpy as np
        BS, SEQ, D_MODEL = (4, 256, 1024)
        N_Q_HEADS, N_KV_HEADS, D_K, D_V = (32, 8, 128, 128)
        ROPE_BASE = 10000.0

        def _rotate_half(x):
            x1, x2 = jnp.split(x, 2, axis=-1)
            return jnp.concatenate([-x2, x1], axis=-1)

        def _apply_rope(x, pos0):
            d = x.shape[-1]
            seq = x.shape[2]
            inv_freq = 1.0 / ROPE_BASE ** (jnp.arange(0, d, 2, dtype=jnp.float32) / d)
            pos = (pos0 + jnp.arange(seq)).astype(jnp.float32)
            ang = pos[:, None] * inv_freq[None, :]
            cos = jnp.concatenate([jnp.cos(ang), jnp.cos(ang)], axis=-1)
            sin = jnp.concatenate([jnp.sin(ang), jnp.sin(ang)], axis=-1)
            return x * cos[None, None] + _rotate_half(x) * sin[None, None]
        bs, sq, _ = query.shape
        n_groups = N_Q_HEADS // N_KV_HEADS
        q = (query @ wq).reshape(bs, sq, N_Q_HEADS, D_K).transpose((0, 2, 1, 3))
        sk = key.shape[1]
        k = (key @ wk).reshape(bs, sk, N_KV_HEADS, 1, D_K)
        k = jnp.repeat(k, n_groups, axis=3).reshape(bs, sk, N_Q_HEADS, D_K).transpose((0, 2, 1, 3))
        v = (value @ wv).reshape(bs, sk, N_KV_HEADS, 1, D_V)
        v = jnp.repeat(v, n_groups, axis=3).reshape(bs, sk, N_Q_HEADS, D_V).transpose((0, 2, 1, 3))
        scale = jnp.sqrt(jnp.float32(D_K))
        q = _apply_rope(q, curr_seq_pos)
        k = _apply_rope(k, curr_seq_pos)
        raw = jnp.einsum('bhqd,bhkd->bhqk', q, k) / scale
        masked = raw + mask[:bs, None, curr_seq_pos:curr_seq_pos + sq, :sk]
        attn = jax.nn.softmax(masked, axis=-1)
        out = jnp.einsum('bhqk,bhkd->bhqd', attn, v)
        out = out.transpose((0, 2, 1, 3)).reshape(bs, sq, N_Q_HEADS * D_V)
        return out @ wo

    def _L0_attn_ref(x):
        import jax, jax.numpy as jnp
        import numpy as np
        import math
        FACTOR = 1
        B, C, L = x.shape
        xh = x[:, None]
        f = jnp.fft.rfft(xh, axis=-1)
        corr = jnp.fft.irfft(f * jnp.conj(f), n=L, axis=-1)
        top_k = int(FACTOR * math.log(L))
        weights, delay = jax.lax.top_k(corr, top_k)
        tmp_corr = jax.nn.softmax(weights, axis=-1)
        init_index = jnp.arange(L)
        idx = (init_index[None, None, None, None, :] + delay[..., None]) % L
        pattern = jnp.take_along_axis(xh[:, :, :, None, :], idx, axis=-1)
        delays_agg = jnp.sum(pattern * tmp_corr[..., None], axis=-2)
        return delays_agg[:, 0]

    def _L0_ffn_ref(x, A, B, Wr):
        import jax, jax.numpy as jnp
        import numpy as np
        LORA_R = 16
        SCALE = 16.0 / np.sqrt(16.0)
        NUM_EXPERTS = 4
        TOP_K = 2
        IN_F = 1024
        OUT_F = 1024
        orig_shape = x.shape
        flat = x.reshape(-1, orig_shape[-1])
        logits = flat @ Wr.T
        topk_vals, topk_idx = jax.lax.top_k(logits, TOP_K)
        T = flat.shape[0]
        neg_inf = jnp.finfo(logits.dtype).min
        sparse = jnp.full_like(logits, neg_inf)
        rows = jnp.arange(T)[:, None]
        sparse = sparse.at[rows, topk_idx].set(topk_vals)
        gates = jax.nn.softmax(sparse, axis=-1)
        mid = jnp.einsum('tf,erf->ter', flat, A)
        all_deltas = jnp.einsum('ter,eor->teo', mid, B) * SCALE
        delta = jnp.sum(gates[:, :, None] * all_deltas, axis=1)
        return delta.reshape(*orig_shape[:-1], -1)
    x = x + _L0_xattn_ref(_layernorm(x, axis=-1), ctx_4096, ctx_4096, mask_BxSxS2_ff0, L0_xattn_wq, L0_xattn_wk, L0_xattn_wv, L0_xattn_wo, 0)
    x = x + _L0_attn_ref(_layernorm(x, axis=-1))
    x = x + _L0_ffn_ref(_layernorm(x, axis=-1), L0_ffn_A, L0_ffn_B, L0_ffn_Wr)
    return x

_drawn_inputs = setup_inputs


def setup_inputs(seed=0):
    import zlib

    import numpy as np

    out = dict(_drawn_inputs(seed))
    spreads = {}
    factors = {}
    for name, (base, spread) in spreads.items():
        noise = np.random.default_rng([zlib.crc32(name.encode()), seed]).standard_normal(out[name].shape)
        drawn = base * np.exp(spread * noise) if base else spread * noise
        out[name] = jnp.asarray(drawn.astype(out[name].dtype))
    for name, factor in factors.items():
        out[name] = (out[name] * factor).astype(out[name].dtype)
    return out
```

```python
from contextlib import ExitStack

import numpy as np

import concourse.bass as bass
from concourse import mybir

ALU = mybir.AluOpType
ACT = mybir.ActivationFunctionType
F32 = mybir.dt.float32
F32R = mybir.dt.float32r
I32 = mybir.dt.int32
U32 = mybir.dt.uint32

P = 128
B, SQ, D = 2, 64, 1024
SK = 1024
HQ, HKV, DK = 32, 8, 128
G = HQ // HKV
T = B * SQ
CH = D // P
UW = 512
KB = SK // UW
STEPS = B * HKV
RING = 6
HALF = D // 2
LAGS = HALF // 2 + 2
SLOT = max(UW, 2 * LAGS)
E, R = 4, 16
LORA_SCALE = 16.0 / np.sqrt(16.0)
EPS = 1e-5
TOPK = 6
LOWEST = -3.0e38

WK_U, WV_U, W_U, CTX_U = 2, 2, 8, KB * CH
FIRST_CTX = WK_U
FIRST_WV = FIRST_CTX + CTX_U
FIRST_W = FIRST_WV + WV_U
FIRST_WK1 = FIRST_W + W_U
FIRST_WV1 = FIRST_WK1 + WK_U
PRO_U = FIRST_WV1 + WV_U
STEP_U = W_U + WK_U + WV_U
CTX1 = PRO_U + STEP_U * (HKV - 1)
STEP7_U = CTX1 + CTX_U
BASE1 = STEP7_U + WK_U + WV_U
STEP14_U = BASE1 + STEP_U * (HKV - 2)
STEP15_U = STEP14_U + W_U
TAB_U = STEP15_U + W_U
assert STEP_U % RING == 0


def step_units(s):
    return (s.first, s.slope)


class Step:

    def __init__(self, s, at):
        self.s, self.at = s, at
        self.batch = at // HKV
        if at < HKV - 1:
            self.first = PRO_U
            self.slope = STEP_U
        elif at == HKV - 1:
            self.first, self.slope = STEP7_U, 0
        elif at <= STEPS - 2:
            self.first, self.slope = BASE1 - STEP_U * HKV, STEP_U
        else:
            self.first, self.slope = STEP15_U, 0

    def unit(self, j):
        return Unit(self.first + j, self.slope, self.s)


class Unit:

    def __init__(self, static, slope=0, s=0):
        self.static, self.slope, self.s = static, slope, s
        self.slot = static % RING

    def count(self, plus):
        return self.static + plus + (self.slope * self.s if self.slope else 0)

    def arrivals(self):
        return 16 * (self.static // RING + 1) + (16 * (self.slope // RING) * self.s if self.slope else 0)


def perceiver_kernel(nc, x, ctx_u, mask, wkv_u, wq_u, wo_u, tab_f, tab_i, cos_k, sin_k, cos_q, sin_q,
                     ident_d, aw, bt, iota_d, out):
    with ExitStack() as stack:
        def sb(name, cols, dt=F32, rows=P):
            return stack.enter_context(nc.sbuf_tensor(name, [rows, cols], dt))

        def pb(name):
            return stack.enter_context(nc.psum_tensor(name, [P, 2 * UW], F32))

        def sem(name):
            return stack.enter_context(nc.semaphore(name))

        ctx_hi, ctx_lo = sb("ctx_hi", CTX_U * UW, F32R), sb("ctx_lo", CTX_U * UW, F32R)
        wk_hi, wk_lo = sb("wk_hi", CH * P, F32R), sb("wk_lo", CH * P, F32R)
        wv_hi, wv_lo = sb("wv_hi", CH * P, F32R), sb("wv_lo", CH * P, F32R)
        w_hi, w_lo = sb("w_hi", W_U * UW, F32R), sb("w_lo", W_U * UW, F32R)
        raw = sb("raw", RING * SLOT)
        k_hi, k_lo = sb("k_hi", SK, F32R), sb("k_lo", SK, F32R)
        v_hi, v_lo = sb("v_hi", SK, F32R), sb("v_lo", SK, F32R)
        soft = sb("soft", 2 * SK)
        pt_hi, pt_lo = sb("pt_hi", 2 * UW, F32R), sb("pt_lo", 2 * UW, F32R)
        cosk, sink = sb("cosk", SK), sb("sink", SK)
        cosq, sinq = sb("cosq", DK), sb("sinq", DK)
        maskt = sb("maskt", SK)
        q1 = sb("q1", HKV * G * SQ)
        o0 = sb("o0", HKV * G * SQ)
        q_hi, q_lo = sb("q_hi", G * SQ, F32R), sb("q_lo", G * SQ, F32R)
        o_hi, o_lo = sb("o_hi", G * T, F32R), sb("o_lo", G * T, F32R)
        xt_hi, xt_lo = sb("xt_hi", CH * T, F32R), sb("xt_lo", CH * T, F32R)
        krot, kswap = sb("krot", KB * UW), sb("kswap", UW)
        ident = sb("ident", P)
        ones = sb("ones", 2)
        st = sb("st", 112)
        top8 = sb("top8", 8)
        flag_i = sb("flag_i", 2, I32)
        idx8 = sb("idx8", 8, U32)

        mx, nm, rs, ri = st[:, 0:4], st[:, 4:6], st[:, 6:8], st[:, 8:10]
        bn, ag, rstd, nbias = st[:, 10:22], st[:, 22:24], st[:, 24:25], st[:, 25:26]
        gap, near = st[:, 26:27], st[:, 27:28]
        lg, ex, sel, gs = st[:, 28:36], st[:, 36:40], st[:, 40:48], st[:, 48:52]
        idxf, iota4 = st[:, 52:60], st[:, 60:64]
        gate = st[:, 108:112]
        ve, sd, rec, nwt = st[:, 104:105], st[:, 105:106], st[:, 106:107], st[:, 107:108]
        neg0, e8 = st[:, 94:95], st[:, 96:104]
        gsum, grec = st[:, 64:65], st[:, 65:66]

        pk = pb("pk")
        pa = pb("pa")
        ps = pb("ps")
        py = pb("py")

        raw_in = [sem(f"raw_in{i}") for i in range(RING)]
        x_in, tab_in, mask_in, late_in, out_done = (sem(n) for n in ("x_in", "tab_in", "mask_in", "late_in", "out_done"))
        unit_hi, unit_lo = sem("unit_hi"), sem("unit_lo")
        ones_set = sem("ones_set")
        ln_bn, ln_ag, ln_var, ln_rstd, ln_out = (sem(n) for n in ("ln_bn", "ln_ag", "ln_var", "ln_rstd", "ln_out"))
        ln_sd = sem("ln_sd")
        xt_ps, xt_h, xt_l, seeded = sem("xt_ps"), sem("xt_h"), sem("xt_l"), sem("seeded")
        kproj, k_mul, k_rot, k_h, k_l = sem("kproj"), sem("k_mul"), sem("k_rot"), sem("k_h"), sem("k_l")
        vproj, vt_raw, vtr, v_h, v_l = sem("vproj"), sem("vt_raw"), sem("vtr"), sem("v_h"), sem("v_l")
        qproj, q_mul, q_rot, qtr, q_h, q_l = (sem(n) for n in ("qproj", "q_mul", "q_rot", "qtr", "q_h", "q_l"))
        scored, masked, nmax, expd, recip, prob = (sem(n) for n in ("scored", "masked", "nmax", "expd", "recip", "prob"))
        ptr, pt_h, pt_l, pv = sem("ptr"), sem("pt_h"), sem("pt_l"), sem("pv")
        o_raw, o_h, o_l, w_used = sem("o_raw"), sem("o_h"), sem("o_l"), sem("w_used")
        fold, ab_ps, ab_h, ab_l, dft = sem("fold"), sem("ab_ps"), sem("ab_h"), sem("ab_l"), sem("dft")
        sq, sq_ps, sq_h, sq_l, idft = sem("sq"), sem("sq_ps"), sem("sq_h"), sem("sq_l"), sem("idft")
        even_out, lagged, topped, gapped, near_ps, flagged = (
            sem(n) for n in ("even_out", "lagged", "topped", "gapped", "near_ps", "flagged"))
        x2_done, h_ps, h_t, lora, lg_in, lg_top, g_exp, g_step, mid_ps, mid_t, delta, y_out = (
            sem(n) for n in ("x2_done", "h_ps", "h_t", "lora", "lg_in", "lg_top", "g_exp", "g_step", "mid_ps",
                             "mid_t", "delta", "y_out"))
        h_t1 = sem("h_t1")
        weighed = sem("weighed")
        gen = sem("gen")

        def raw_ap(u, cols=UW):
            return raw[:, u.slot * SLOT:u.slot * SLOT + cols]

        def blk(t, i, w=UW):
            return t[:, i * w:(i + 1) * w]

        block = stack.enter_context(nc.Block())

        @block.sync
        def _(sp):
            def load_unit(u, src, cols=UW, wait=True):
                if wait:
                    sp.wait_ge(unit_lo, u.count(1 - RING))
                sp.dma_start(raw_ap(u, cols), src).then_inc(raw_in[u.slot], 16)

            def load_pro(n, src):
                load_unit(Unit(n), src, wait=n >= RING)

            def load_wkv(step, j0, head, j):
                for i in range(2):
                    load_unit(step.unit(j0 + i), wkv_u[head, 2 * j + i])

            def load_w(step, table, head):
                for j in range(W_U):
                    load_unit(step.unit(j), table[head, j])

            def load_mask(b):
                for h in range(2):
                    sp.dma_start(maskt[h * SQ:(h + 1) * SQ, :], mask[b]).then_inc(mask_in, 16)

            for i in range(WK_U):
                load_pro(i, wkv_u[0, i])
            for i in range(4):
                load_pro(FIRST_CTX + i, ctx_u[0, i])
            sp.dma_start(soft[:, 0:D], x).then_inc(x_in, 16)
            sp.dma_start(ident[:, :], ident_d).then_inc(x_in, 16)
            for i in range(4, CTX_U):
                load_pro(FIRST_CTX + i, ctx_u[0, i])
                if i == CH - 1:
                    sp.dma_start(cosk[:, :], cos_k).then_inc(tab_in, 16)
                    sp.dma_start(sink[:, :], sin_k).then_inc(tab_in, 16)
            for i in range(WV_U):
                load_pro(FIRST_WV + i, wkv_u[0, 2 + i])
            sp.dma_start(cosq[:, :], cos_q).then_inc(tab_in, 16)
            sp.dma_start(sinq[:, :], sin_q).then_inc(tab_in, 16)
            for i in range(W_U):
                load_pro(FIRST_W + i, wq_u[0, i])
            load_mask(0)
            for i in range(WK_U + WV_U):
                load_pro(FIRST_WK1 + i, wkv_u[1, i])

            with sp.Fori(0, HKV - 2) as s:
                step = Step(s, 0)
                load_w(step, wq_u, s + 1)
                load_wkv(step, W_U, s + 2, 0)
                load_wkv(step, W_U + 2, s + 2, 1)
            step = Step(HKV - 2, HKV - 2)
            load_w(step, wq_u, HKV - 1)
            load_wkv(step, W_U, 0, 0)
            load_wkv(step, W_U + 2, 0, 1)
            for i in range(CTX_U):
                load_unit(Unit(CTX1 + i), ctx_u[1, i])
            step = Step(HKV - 1, HKV - 1)
            load_wkv(step, 0, 1, 0)
            load_wkv(step, 2, 1, 1)
            sp.wait_ge(masked, 4 * HKV)
            load_mask(1)
            with sp.Fori(HKV, STEPS - 2) as s:
                step = Step(s, HKV)
                load_w(step, wo_u, s - HKV)
                load_wkv(step, W_U, s - HKV + 2, 0)
                load_wkv(step, W_U + 2, s - HKV + 2, 1)
            load_w(Step(STEPS - 2, STEPS - 2), wo_u, HKV - 2)
            load_w(Step(STEPS - 1, STEPS - 1), wo_u, HKV - 1)
            sp.wait_ge(k_rot, KB * STEPS)
            sp.dma_start(cosk[0:E * R, :], bt).then_inc(late_in, 16)
            sp.dma_start(sink[:, 0:CH * (E + E * R)], aw).then_inc(late_in, 16)
            sp.dma_start(iota4, iota_d).then_inc(late_in, 16)
            for i in range(8):
                load_unit(Unit(TAB_U + i), tab_f[i])
            for i in range(4):
                load_unit(Unit(TAB_U + 8 + i), tab_i[i], 2 * LAGS)
            for i in range(2):
                sp.wait_ge(y_out, i + 1)
                sp.dma_start(out[:, i * UW:(i + 1) * UW], blk(soft, i)).then_inc(out_done, 16)
            sp.wait_ge(out_done, 32)

        @block.tensor
        def _(pe):
            def product(acc, st_hi, st_lo, mv_hi, mv_lo, first, last):
                nc.tensor.matmul(acc, st_lo, mv_hi, start=first, stop=False)
                nc.tensor.matmul(acc, st_hi, mv_lo, start=False, stop=False)
                return nc.tensor.matmul(acc, st_hi, mv_hi, start=False, stop=last)

            def project(acc, hi, lo, b, units=None):
                for c in range(CH):
                    if units is not None:
                        pe.wait_ge(unit_lo, units + c + 1)
                    mm = product(acc, blk(hi, c, P), blk(lo, c, P), blk(ctx_hi, b * CH + c),
                                 blk(ctx_lo, b * CH + c), c == 0, c == CH - 1)
                return mm

            def k_project(m, wk_ready, ctx_first=None, again=True):
                pe.wait_ge(unit_lo, wk_ready)
                for b in range(KB):
                    if again:
                        pe.wait_ge(k_rot, KB * m + b - 1)
                    project(blk(pk, b), wk_hi, wk_lo, b,
                            None if ctx_first is None else ctx_first + CH * b).then_inc(kproj, 1)

            def v_project(m, wv_ready, again=True):
                pe.wait_ge(unit_lo, wv_ready)
                for b in range(KB):
                    if again:
                        pe.wait_ge(pt_l, 4 * m + b - 1)
                    project(blk(pa, b), wv_hi, wv_lo, b).then_inc(vproj, 1)

            def v_transposes(m):
                for b in range(KB):
                    pe.wait_ge(vt_raw, KB * m + b + 1)
                    for c in range(4):
                        mm = nc.tensor.transpose(pa[:, b * UW + c * P:b * UW + (c + 1) * P],
                                                 soft[:, b * UW + c * P:b * UW + (c + 1) * P], ident[:, :])
                    mm.then_inc(vtr, 1)

            def q_project(m, unit, again=True):
                if again:
                    pe.wait_ge(masked, 4 * m)
                for c in range(CH):
                    pe.wait_ge(unit_lo, unit.count(c + 1))
                    mm = product(blk(ps, 1), blk(xt_hi, c, P), blk(xt_lo, c, P), blk(w_hi, c), blk(w_lo, c),
                                 c == 0, c == CH - 1)
                mm.then_inc(qproj, 1)

            def q_transposes(m, again=True):
                pe.wait_ge(q_rot, m + 1)
                if again:
                    pe.wait_ge(o_raw, m)
                for h in range(G):
                    mm = nc.tensor.transpose(blk(ps, h, P), soft[:, SK + h * P:SK + (h + 1) * P], ident[:, :])
                mm.then_inc(qtr, 1)

            def scores(s):
                pe.wait_ge(q_l, s + 1)
                pe.wait_ge(k_l, KB * s + 2)
                for i in range(4):
                    t, b = divmod(i, 2)
                    if i >= 2:
                        pe.wait_ge(masked, 4 * s + i - 1)
                    product(blk(ps, b), blk(q_hi, t, P), blk(q_lo, t, P), blk(k_hi, b), blk(k_lo, b),
                            True, True).then_inc(scored, 1)

            def attend(s):
                def turn(i):
                    if i < 2:
                        pe.wait_ge(v_l, KB * s + i + 1)
                    else:
                        pe.wait_ge(pt_l, 4 * s + i - 1)
                    for c in range(2):
                        for t in range(2):
                            mm = nc.tensor.transpose(
                                pa[:, (i % 2) * UW + c * 256 + t * P:(i % 2) * UW + c * 256 + (t + 1) * P],
                                soft[:, t * SK + (2 * i + c) * P:t * SK + (2 * i + c + 1) * P], ident[:, :])
                    mm.then_inc(ptr, 1)

                def weigh(i):
                    pe.wait_ge(pt_l, 4 * s + i + 1)
                    if i == 0:
                        pe.wait_ge(v_l, KB * s + 2)
                    for c in range(2):
                        k, m = 2 * i + c, (i % 2) * UW + c * 256
                        mm = product(ps[:, 0:G * SQ], blk(v_hi, k, P), blk(v_lo, k, P), pt_hi[:, m:m + 256],
                                     pt_lo[:, m:m + 256], k == 0, k == CH - 1)
                    mm.then_inc(pv, 1)

                pe.wait_ge(prob, 2 * s + 2)
                for i in range(4):
                    turn(i)
                    if i >= 1:
                        weigh(i - 1)
                weigh(3)

            def out_project(s, unit, final):
                pe.wait_ge(o_l, s - HKV + 1)
                for j in range(W_U):
                    h, n = divmod(j, 2)
                    pe.wait_ge(unit_lo, unit.count(j + 1))
                    mm = product(blk(py, n), blk(o_hi, h, T), blk(o_lo, h, T), blk(w_hi, j), blk(w_lo, j),
                                 False, final and h == G - 1)
                mm.then_inc(w_used, 1)

            k_project(0, WK_U, FIRST_CTX, again=False)
            pe.wait_ge(x_in, 32)
            for n in range(2):
                mm = nc.tensor.matmul(blk(py, n), ident[:, :], blk(soft, n), start=True, stop=False)
            mm.then_inc(seeded, 1)
            pe.wait_ge(ln_out, 1)
            for n in range(2):
                for c in range(4):
                    mm = nc.tensor.transpose(ps[:, n * UW + c * P:n * UW + (c + 1) * P],
                                             soft[:, D + n * UW + c * P:D + n * UW + (c + 1) * P], ident[:, :])
                mm.then_inc(xt_ps, 1)
            v_project(0, FIRST_WV + WV_U, again=False)
            pe.wait_ge(xt_l, 2)
            q_project(0, Unit(FIRST_W), again=False)
            v_transposes(0)
            q_transposes(0, again=False)

            def step_0(s, at):
                step = Step(s, at)
                scores(s)
                k_project(s + 1, step.unit(0).count(-WV_U))
                attend(s)
                v_project(s + 1, step.unit(0).count(0))
                q_project(s + 1, step.unit(0))
                v_transposes(s + 1)
                q_transposes(s + 1)

            with pe.Fori(0, HKV - 2) as s:
                step_0(s, 0)
            step_0(HKV - 2, HKV - 2)
            s = HKV - 1
            scores(s)
            k_project(s + 1, CTX1, CTX1)
            attend(s)
            v_project(s + 1, CTX1)
            v_transposes(s + 1)

            def step_1(s, at, more):
                step = Step(s, at)
                scores(s)
                if more:
                    k_project(s + 1, step.unit(0).count(-WV_U))
                attend(s)
                if more:
                    v_project(s + 1, step.unit(0).count(0))
                    v_transposes(s + 1)
                out_project(s, step.unit(0), final=not more)

            with pe.Fori(HKV, STEPS - 2) as s:
                step_1(s, HKV, True)
            step_1(STEPS - 2, STEPS - 2, True)
            step_1(STEPS - 1, STEPS - 1, False)

            def transposes(dst, src, done):
                for n in range(2):
                    for c in range(4):
                        at = n * UW + c * P
                        mm = nc.tensor.transpose(dst[:, at:at + P], src[:, at:at + P], ident[:, :])
                    mm.then_inc(done, 1)

            pe.wait_ge(fold, 2)
            transposes(pk, q1[:, D:2 * D], ab_ps)
            pe.wait_ge(unit_lo, TAB_U + 8)
            for n in range(2):
                pe.wait_ge(ab_l, n + 1)
                for c in range(4):
                    j = 4 * n + c
                    mm = product(blk(pa, n), blk(xt_hi, j, P), blk(xt_lo, j, P), blk(ctx_hi, j), blk(ctx_lo, j),
                                 c == 0, c == 3)
                mm.then_inc(dft, 1)
            pe.wait_ge(sq, 2)
            transposes(pk, o0[:, 0:D], sq_ps)
            pe.wait_ge(unit_lo, TAB_U + 12)
            for n in range(2):
                pe.wait_ge(sq_l, n + 1)
                for c in range(4):
                    j = 4 * n + c
                    at = 8 * UW + j * LAGS
                    mm = product(ps[:, n * UW:n * UW + LAGS], blk(k_hi, j, P), blk(k_lo, j, P),
                                 ctx_hi[:, at:at + LAGS], ctx_lo[:, at:at + LAGS], c == 0, c == 3)
                mm.then_inc(idft, 1)
            pe.wait_ge(gapped, 3)
            nc.tensor.matmul(pk[0:1, 0:1], near, ones[:, 0:1], start=True, stop=True).then_inc(near_ps, 1)
            pe.wait_ge(ln_out, 3)
            pe.wait_ge(flagged, 1)
            transposes(pk, soft[:, D:2 * D], h_ps)
            pe.wait_ge(late_in, 48)
            W = E + E * R
            for c in range(CH):
                if c % 4 == 0:
                    pe.wait_ge((h_t, h_t1)[c // 4], 1)
                mm = nc.tensor.matmul(ps[:, 0:W], blk(maskt, c, P), sink[:, c * W:(c + 1) * W],
                                      start=c == 0, stop=c == CH - 1)
            mm.then_inc(lora, 1)
            pe.wait_ge(g_step, 6)
            nc.tensor.transpose(ps[0:E * R, UW:UW + P], krot[:, 0:E * R], ident[:, :]).then_inc(mid_ps, 1)
            pe.wait_ge(mid_t, 1)
            for n in range(2):
                nc.tensor.matmul(blk(pa, n), krot[0:E * R, 128:256], cosk[0:E * R, n * UW:(n + 1) * UW],
                                 start=True, stop=True).then_inc(delta, 1)

        @block.scalar
        def _(act):
            def unit(u, dst, free=None, cols=UW):
                if free is not None:
                    act.wait_ge(*free)
                act.wait_ge(raw_in[u.slot], u.arrivals())
                nc.scalar.copy(dst, raw_ap(u, cols)).then_inc(unit_hi, 1)

            def root(n):
                act.wait_ge(ln_var, n)
                nc.scalar.activation(sd, ve, ACT.Sqrt).then_inc(ln_sd, 1)

            def k_his(m, again=True):
                for b in range(KB):
                    act.wait_ge(k_rot, KB * m + b + 1)
                    if again:
                        act.wait_ge(scored, 4 * m)
                    nc.scalar.copy(blk(k_hi, b), blk(krot, b)).then_inc(k_h, 1)

            def vt_raws(m, again=True):
                for b in range(KB):
                    act.wait_ge(vproj, KB * m + b + 1)
                    if again:
                        act.wait_ge(ptr, 4 * m)
                    nc.scalar.copy(blk(soft, b), blk(pa, b)).then_inc(vt_raw, 1)

            def v_his(m, again=True):
                for b in range(KB):
                    act.wait_ge(vtr, KB * m + b + 1)
                    if again:
                        act.wait_ge(pv, 4 * m)
                    nc.scalar.copy(blk(v_hi, b), blk(pa, b)).then_inc(v_h, 1)

            def q_his_0(m, again=True):
                act.wait_ge(qtr, m + 1)
                if again:
                    act.wait_ge(scored, 4 * m)
                src = blk(ps, 0).rearrange("p (h b t) -> p b h t", h=G, b=B)
                nc.scalar.copy(q_hi.rearrange("p (h t) -> p h t", h=G), src[:, 0]).then_inc(q_h, 1)
                nc.scalar.copy(q1[:, bass.ds(m * (G * SQ), G * SQ)].rearrange("p (h t) -> p h t", h=G),
                               src[:, 1]).then_inc(q_h, 1)

            def q_his_1(m):
                act.wait_ge(scored, 4 * m)
                nc.scalar.copy(q_hi[:, :], q1[:, bass.ds((m - HKV) * (G * SQ), G * SQ)]).then_inc(q_h, 2)

            def softmax_exp(s):
                for t in range(2):
                    act.wait_ge(nmax, 2 * s + t + 1)
                    nc.scalar.activation(blk(soft, t, SK), blk(soft, t, SK), ACT.Exp, bias=nm[:, t:t + 1],
                                         scale=1.0, accum_out=rs[:, t:t + 1]).then_inc(expd, 1)

            def w_units(step, free):
                for j in range(W_U):
                    unit(step.unit(j), blk(w_hi, j), free if j == 0 else None)

            def pt_his(s, first):
                for i in range(4):
                    act.wait_ge(ptr, 4 * s + i + 1)
                    if i >= 2 or not first:
                        act.wait_ge(pv, 4 * s + i - 1)
                    nc.scalar.copy(blk(pt_hi, i % 2), blk(pa, i % 2)).then_inc(pt_h, 1)

            def attend_0(s, first=False):
                pt_his(s, first)
                act.wait_ge(pv, 4 * s + 4)
                nc.scalar.copy(o0[:, bass.ds(s * (G * SQ), G * SQ)], ps[:, 0:G * SQ]).then_inc(o_raw, 1)

            def attend_1(s):
                oh = o_hi.rearrange("p (h b t) -> p b h t", h=G, b=B)
                act.wait_ge(w_used, s - HKV)
                nc.scalar.copy(oh[:, 0], o0[:, bass.ds((s - HKV) * (G * SQ), G * SQ)]
                               .rearrange("p (h t) -> p h t", h=G)).then_inc(o_h, 1)
                pt_his(s, False)
                act.wait_ge(pv, 4 * s + 4)
                nc.scalar.copy(oh[:, 1], ps[:, 0:G * SQ].rearrange("p (h t) -> p h t", h=G)).then_inc(o_h, 1)

            def next_k(s, step, j0):
                k_his(s + 1)
                for j in range(WK_U):
                    unit(step.unit(j0 + j), blk(wk_hi, j), (kproj, KB * (s + 2)) if j == 0 else None)

            def next_v(s, step, j0):
                vt_raws(s + 1)
                for j in range(WV_U):
                    unit(step.unit(j0 + j), blk(wv_hi, j), (vproj, KB * (s + 2)) if j == 0 else None)

            for j in range(WK_U):
                unit(Unit(j), blk(wk_hi, j))
            for j in range(CTX_U):
                unit(Unit(FIRST_CTX + j), blk(ctx_hi, j))
                if j == CH - 1:
                    root(1)
            for j in range(WV_U):
                unit(Unit(FIRST_WV + j), blk(wv_hi, j))
            for n in range(2):
                act.wait_ge(xt_ps, n + 1)
                nc.scalar.copy(blk(xt_hi, n), blk(ps, n)).then_inc(xt_h, 1)
            k_his(0, again=False)
            for j in range(W_U):
                unit(Unit(FIRST_W + j), blk(w_hi, j))
            for j in range(WK_U):
                unit(Unit(FIRST_WK1 + j), blk(wk_hi, j), (kproj, KB))
            act.wait_ge(seeded, 1)
            act.wait_ge(ln_out, 1)
            vt_raws(0, again=False)
            for j in range(WV_U):
                unit(Unit(FIRST_WV1 + j), blk(wv_hi, j), (vproj, KB))
            q_his_0(0, again=False)

            def step_0(s, at, first=False):
                step = Step(s, at)
                softmax_exp(s)
                v_his(s, again=not first)
                w_units(step, (qproj, s + 1))
                attend_0(s, first)
                next_k(s, step, W_U)
                next_v(s, step, W_U + WK_U)
                q_his_0(s + 1)

            step_0(0, 0, True)
            with act.Fori(1, HKV - 2) as s:
                step_0(s, 0)
            step_0(HKV - 2, HKV - 2)
            s = HKV - 1
            for j in range(CTX_U):
                unit(Unit(CTX1 + j), blk(ctx_hi, j), (vproj, KB * (s + 1)) if j == 0 else None)
            step = Step(s, s)
            softmax_exp(s)
            v_his(s)
            attend_0(s)
            next_k(s, step, 0)
            next_v(s, step, WK_U)
            act.wait_ge(q_h, 2 * HKV)
            q_his_1(s + 1)

            def step_1(s, at, k=True, wkv=True):
                step = Step(s, at)
                softmax_exp(s)
                v_his(s)
                act.wait_ge(qproj, HKV)
                w_units(step, (w_used, s - HKV))
                attend_1(s)
                if wkv:
                    next_k(s, step, W_U)
                    next_v(s, step, W_U + WK_U)
                elif k:
                    k_his(s + 1)
                    vt_raws(s + 1)
                if k:
                    q_his_1(s + 1)

            with act.Fori(HKV, STEPS - 2) as s:
                step_1(s, HKV)
            step_1(STEPS - 2, STEPS - 2, wkv=False)
            step_1(STEPS - 1, STEPS - 1, k=False, wkv=False)
            for j in range(8):
                unit(Unit(TAB_U + j), blk(ctx_hi, j))
            for j in range(4):
                at = 8 * UW + 2 * j * LAGS
                unit(Unit(TAB_U + 8 + j), ctx_hi[:, at:at + 2 * LAGS], cols=2 * LAGS)

            root(2)
            for n in range(2):
                act.wait_ge(ab_ps, n + 1)
                nc.scalar.copy(blk(xt_hi, n), blk(pk, n)).then_inc(ab_h, 1)
            for n in range(2):
                act.wait_ge(dft, n + 1)
                nc.scalar.activation(blk(o0, n), blk(pa, n), ACT.Square).then_inc(sq, 1)
            for n in range(2):
                act.wait_ge(sq_ps, n + 1)
                nc.scalar.copy(blk(k_hi, n), blk(pk, n)).then_inc(sq_h, 1)
            act.wait_ge(idft, 1)
            nc.scalar.copy(krot[:, 0:LAGS], ps[:, 0:LAGS]).then_inc(even_out, 1)
            act.wait_ge(gapped, 1)
            nc.scalar.activation(e8, top8[:, :], ACT.Exp, bias=neg0, scale=1.0).then_inc(weighed, 1)
            root(3)
            act.wait_ge(h_ps, 1)
            nc.scalar.copy(blk(maskt, 0), blk(pk, 0)).then_inc(h_t, 1)
            act.wait_ge(lg_top, 1)
            nc.scalar.activation(ex, lg[:, 0:E], ACT.Exp, bias=gap, scale=1.0).then_inc(g_exp, 1)

        @block.vector
        def _(dve):
            def unit(u, dst_hi, dst_lo, cols=UW):
                dve.wait_ge(unit_hi, u.count(1))
                nc.vector.tensor_tensor(dst_lo, raw_ap(u, cols), dst_hi, ALU.subtract).then_inc(unit_lo, 1)

            def lo(dst_lo, src, hi, done, ready=None):
                if ready is not None:
                    dve.wait_ge(*ready)
                nc.vector.tensor_tensor(dst_lo, src, hi, ALU.subtract).then_inc(done, 1)

            def layer_norm(src, dst, n):
                for h in range(2):
                    nc.vector.bn_stats(bn[:, 6 * h:6 * h + 6], blk(src, h)).then_inc(ln_bn, 1)
                dve.wait_ge(ln_bn, 2 * n)
                nc.vector.bn_aggr(ag, bn).then_inc(ln_ag, 1)
                dve.wait_ge(ln_ag, n)
                nc.vector.tensor_scalar(ve, ag[:, 1:2], EPS, None, ALU.add).then_inc(ln_var, 1)
                dve.wait_ge(ln_sd, n)
                nc.vector.reciprocal(rec, sd).then_inc(ln_rstd, 1)
                dve.wait_ge(ln_rstd, 4 * n - 3)
                nc.vector.scalar_tensor_tensor(out=nwt, in0=rec, scalar=rec, in1=ve, op0=ALU.mult,
                                               op1=ALU.mult).then_inc(ln_rstd, 1)
                dve.wait_ge(ln_rstd, 4 * n - 2)
                nc.vector.tensor_scalar(nwt, nwt, -0.5, 1.5, ALU.mult, ALU.add).then_inc(ln_rstd, 1)
                dve.wait_ge(ln_rstd, 4 * n - 1)
                nc.vector.tensor_tensor(rstd, rec, nwt, ALU.mult).then_inc(ln_rstd, 1)
                dve.wait_ge(ln_rstd, 4 * n)
                nc.vector.tensor_scalar(dst, src, ag[:, 0:1], rstd, ALU.subtract, ALU.mult).then_inc(ln_out, 1)

            def rotate(m, b, again=True):
                dve.wait_ge(kproj, KB * m + b + 1)
                src, cs, sn = blk(pk, b), blk(cosk, b), blk(sink, b)
                nc.vector.tensor_tensor(blk(krot, b), src, cs, ALU.mult).then_inc(k_mul, 1)
                if again:
                    dve.wait_ge(k_rot, KB * m + b)
                nc.vector.tensor_tensor(kswap[0:64, :], src[64:128, :], sn[64:128, :], ALU.mult).then_inc(k_mul, 1)
                nc.vector.tensor_tensor(kswap[64:128, :], src[0:64, :], sn[0:64, :], ALU.mult).then_inc(k_mul, 1)
                dve.wait_ge(k_mul, 3 * (KB * m + b + 1))
                nc.vector.tensor_tensor(blk(krot, b), blk(krot, b), kswap[:, :], ALU.add).then_inc(k_rot, 1)

            def k_los(m):
                for b in range(KB):
                    lo(blk(k_lo, b), blk(krot, b), blk(k_hi, b), k_l, (k_h, KB * m + b + 1))

            def v_los(m):
                for b in range(KB):
                    lo(blk(v_lo, b), blk(pa, b), blk(v_hi, b), v_l, (v_h, KB * m + b + 1))

            def rotate_q(m):
                dve.wait_ge(qproj, m + 1)
                q = blk(ps, 1).rearrange("p (h two d) -> p h two d", h=G, two=2)
                cos = cosq[:, :].unsqueeze(1).broadcast_to([P, G, DK])
                sin = sinq[:, :].rearrange("p (two d) -> p two d", two=2).unsqueeze(1).broadcast_to([P, G, 2, DK // 2])
                prod = blk(soft, 2)
                swap = blk(soft, 3).rearrange("p (h two d) -> p h two d", h=G, two=2)
                nc.vector.tensor_tensor(prod.rearrange("p (h d) -> p h d", h=G),
                                        blk(ps, 1).rearrange("p (h d) -> p h d", h=G), cos, ALU.mult).then_inc(q_mul, 1)
                for i in range(2):
                    nc.vector.tensor_tensor(swap[:, :, i, :], q[:, :, 1 - i, :], sin[:, :, i, :],
                                            ALU.mult).then_inc(q_mul, 1)
                dve.wait_ge(q_mul, 3 * m + 3)
                nc.vector.tensor_tensor(prod, prod, blk(soft, 3), ALU.add).then_inc(q_rot, 1)

            def q_lo_0(m):
                lo(q_lo.rearrange("p (h t) -> p h t", h=G),
                   blk(ps, 0).rearrange("p (h b t) -> p b h t", h=G, b=B)[:, 0],
                   q_hi.rearrange("p (h t) -> p h t", h=G), q_l, (q_h, 2 * m + 2))

            def q_lo_1(m):
                lo(q_lo[:, :], q1[:, bass.ds((m - HKV) * (G * SQ), G * SQ)], q_hi[:, :], q_l, (q_h, 2 * m + 2))

            def softmax(s, batch):
                for i in range(4):
                    dve.wait_ge(scored, 4 * s + i + 1)
                    nc.vector.memset(gate[:, i:i + 1], 0.0)
                    dve.wait_ge(mask_in, 32 * (batch + 1))
                    nc.vector.tensor_tensor_reduce(
                        out=blk(soft, i), in0=blk(ps, i % 2), in1=blk(maskt, i % 2), scale=1.0, scalar=LOWEST,
                        op0=ALU.add, op1=ALU.max, accum_out=mx[:, i:i + 1]).then_inc(masked, 1)
                    if i % 2:
                        t = i // 2
                        dve.wait_ge(masked, 4 * s + i + 1)
                        nc.vector.tensor_scalar(nm[:, t:t + 1], mx[:, i - 1:i], mx[:, i:i + 1], -1.0,
                                                ALU.max, ALU.mult).then_inc(nmax, 1)

            def divide(s):
                for t in range(2):
                    dve.wait_ge(expd, 2 * s + t + 1)
                    nc.vector.reciprocal(ri[:, t:t + 1], rs[:, t:t + 1]).then_inc(recip, 1)
                    dve.wait_ge(recip, 2 * s + t + 1)
                    nc.vector.tensor_scalar(blk(soft, t, SK), blk(soft, t, SK), ri[:, t:t + 1], None,
                                            ALU.mult).then_inc(prob, 1)

            def pt_los(s):
                for i in range(4):
                    lo(blk(pt_lo, i % 2), blk(pa, i % 2), blk(pt_hi, i % 2), pt_l, (pt_h, 4 * s + i + 1))

            def w_los(step):
                for j in range(W_U):
                    unit(step.unit(j), blk(w_hi, j), blk(w_lo, j))

            def next_k(s, step, j0):
                for b in range(KB):
                    rotate(s + 1, b)
                k_los(s + 1)
                for j in range(WK_U):
                    unit(step.unit(j0 + j), blk(wk_hi, j), blk(wk_lo, j))

            def next_v(step, j0):
                for j in range(WV_U):
                    unit(step.unit(j0 + j), blk(wv_hi, j), blk(wv_lo, j))

            nc.vector.memset(ones[:, :], 1.0).then_inc(ones_set, 1)
            for j in range(WK_U):
                unit(Unit(j), blk(wk_hi, j), blk(wk_lo, j))
            for j in range(CH):
                unit(Unit(FIRST_CTX + j), blk(ctx_hi, j), blk(ctx_lo, j))
            dve.wait_ge(x_in, 32)
            layer_norm(soft[:, 0:D], soft[:, D:2 * D], 1)
            for j in range(CH, CTX_U):
                unit(Unit(FIRST_CTX + j), blk(ctx_hi, j), blk(ctx_lo, j))
            dve.wait_ge(tab_in, 64)
            rotate(0, 0, again=False)
            for j in range(WV_U):
                unit(Unit(FIRST_WV + j), blk(wv_hi, j), blk(wv_lo, j))
            rotate(0, 1)
            for n in range(2):
                lo(blk(xt_lo, n), blk(ps, n), blk(xt_hi, n), xt_l, (xt_h, n + 1))
            k_los(0)
            for j in range(W_U):
                unit(Unit(FIRST_W + j), blk(w_hi, j), blk(w_lo, j))
            for j in range(WK_U):
                unit(Unit(FIRST_WK1 + j), blk(wk_hi, j), blk(wk_lo, j))
            for j in range(WV_U):
                unit(Unit(FIRST_WV1 + j), blk(wv_hi, j), blk(wv_lo, j))
            rotate_q(0)
            q_lo_0(0)

            def step_0(s, at):
                step = Step(s, at)
                dve.wait_ge(vtr, KB * (s + 1))
                dve.wait_ge(qtr, s + 1)
                softmax(s, 0)
                v_los(s)
                divide(s)
                w_los(step)
                pt_los(s)
                next_k(s, step, W_U)
                next_v(step, W_U + WK_U)
                rotate_q(s + 1)
                q_lo_0(s + 1)

            with dve.Fori(0, HKV - 2) as s:
                step_0(s, 0)
            step_0(HKV - 2, HKV - 2)
            s = HKV - 1
            step = Step(s, s)
            for j in range(CTX_U):
                unit(Unit(CTX1 + j), blk(ctx_hi, j), blk(ctx_lo, j))
            dve.wait_ge(vtr, KB * (s + 1))
            dve.wait_ge(qtr, s + 1)
            softmax(s, 0)
            v_los(s)
            divide(s)
            pt_los(s)
            next_k(s, step, 0)
            next_v(step, WK_U)
            q_lo_1(s + 1)

            def step_1(s, at, k=True, wkv=True):
                step = Step(s, at)
                dve.wait_ge(vtr, KB * (s + 1))
                softmax(s, 1)
                v_los(s)
                divide(s)
                w_los(step)
                ol, oh = (t.rearrange("p (h b t) -> p b h t", h=G, b=B) for t in (o_lo, o_hi))
                dve.wait_ge(o_h, 2 * (s - HKV) + 1)
                nc.vector.tensor_tensor(ol[:, 0], o0[:, bass.ds((s - HKV) * (G * SQ), G * SQ)]
                                        .rearrange("p (h t) -> p h t", h=G), oh[:, 0], ALU.subtract)
                pt_los(s)
                lo(ol[:, 1], ps[:, 0:G * SQ].rearrange("p (h t) -> p h t", h=G), oh[:, 1], o_l,
                   (o_h, 2 * (s - HKV) + 2))
                if wkv:
                    next_k(s, step, W_U)
                    next_v(step, W_U + WK_U)
                elif k:
                    for b in range(KB):
                        rotate(s + 1, b)
                    k_los(s + 1)
                if k:
                    q_lo_1(s + 1)

            with dve.Fori(HKV, STEPS - 2) as s:
                step_1(s, HKV)
            step_1(STEPS - 2, STEPS - 2, wkv=False)
            step_1(STEPS - 1, STEPS - 1, k=False, wkv=False)
            for j in range(8):
                unit(Unit(TAB_U + j), blk(ctx_hi, j), blk(ctx_lo, j))
            for j in range(4):
                at = 8 * UW + 2 * j * LAGS
                unit(Unit(TAB_U + 8 + j), ctx_hi[:, at:at + 2 * LAGS], ctx_lo[:, at:at + 2 * LAGS], 2 * LAGS)

            xn, ab = q1[:, 0:D], q1[:, D:2 * D]
            dve.wait_ge(w_used, HKV)
            layer_norm(py[:, :], xn, 2)
            dve.wait_ge(ln_out, 2)
            nc.vector.tensor_tensor(blk(ab, 0), blk(xn, 0), blk(xn, 1), ALU.add).then_inc(fold, 1)
            nc.vector.tensor_tensor(blk(ab, 1), blk(xn, 0), blk(xn, 1), ALU.subtract).then_inc(fold, 1)
            for n in range(2):
                lo(blk(xt_lo, n), blk(pk, n), blk(xt_hi, n), ab_l, (ab_h, n + 1))
            for n in range(2):
                lo(blk(k_lo, n), blk(pk, n), blk(k_hi, n), sq_l, (sq_h, n + 1))
            L0 = HALF // 2 + 1
            corr = o0[:, D:D + HALF + 1]
            dve.wait_ge(idft, 2)
            dve.wait_ge(even_out, 1)
            nc.vector.tensor_tensor(corr[:, 0:L0], krot[:, 0:L0], ps[:, UW:UW + L0], ALU.add).then_inc(lagged, 1)
            nc.vector.tensor_tensor(corr[:, L0:HALF + 1], krot[:, 0:L0 - 1], ps[:, UW:UW + L0 - 1],
                                    ALU.subtract).then_inc(lagged, 1)
            dve.wait_ge(lagged, 2)
            nc.vector.max(top8[:, :], corr).then_inc(topped, 1)
            dve.wait_ge(topped, 1)
            nc.vector.tensor_scalar(neg0, top8[:, 0:1], -1.0, None, ALU.mult).then_inc(gapped, 1)
            nc.vector.tensor_scalar(gap, top8[:, 1:2], top8[:, 0:1], None, ALU.subtract).then_inc(gapped, 1)
            dve.wait_ge(gapped, 2)
            nc.vector.tensor_scalar(near, gap, -110.0, None, ALU.is_ge).then_inc(gapped, 1)
            x2 = soft[:, 0:D]
            nc.vector.tensor_tensor(x2, py[:, :], xn, ALU.add).then_inc(x2_done, 1)
            dve.wait_ge(near_ps, 1)
            nc.vector.tensor_copy(flag_i[0:1, 0:1], pk[0:1, 0:1]).then_inc(flagged, 1)
            dve.wait_ge(flagged, 1)
            dve.wait_ge(x2_done, 1)
            rows_near = dve.value_load(flag_i[0:1, 0:1], min_val=0, max_val=P)
            with dve.If(rows_near > 0):
                dve.wait_ge(weighed, 1)
                delayed_sum(nc, dve, gen, st, e8, top8, idx8, corr, q1, py, x2)
            layer_norm(x2, soft[:, D:2 * D], 3)

            dve.wait_ge(h_ps, 2)
            nc.vector.tensor_copy(blk(maskt, 1), blk(pk, 1)).then_inc(h_t1, 1)
            nc.vector.memset(lg, LOWEST).then_inc(lg_in, 1)
            dve.wait_ge(lg_in, 1)
            dve.wait_ge(lora, 1)
            nc.vector.tensor_copy(lg[:, 0:E], ps[:, 0:E]).then_inc(lg_in, 1)
            dve.wait_ge(lg_in, 2)
            dve.wait_ge(weighed, 1)
            nc.vector.max(top8[:, :], lg).then_inc(topped, 1)
            dve.wait_ge(topped, 2)
            nc.vector.tensor_scalar(gap, top8[:, 0:1], -1.0, None, ALU.mult).then_inc(lg_top, 1)
            nc.vector.max_index(idx8[:, :], top8[:, :], lg).then_inc(g_step, 1)
            dve.wait_ge(g_step, 1)
            nc.vector.tensor_copy(idxf, idx8[:, :]).then_inc(g_step, 1)
            dve.wait_ge(g_step, 2)
            dve.wait_ge(late_in, 48)
            nc.vector.tensor_scalar(sel[:, 0:E], iota4, idxf[:, 0:1], None, ALU.is_equal).then_inc(g_step, 1)
            dve.wait_ge(g_step, 3)
            nc.vector.scalar_tensor_tensor(out=sel[:, E:2 * E], in0=iota4, scalar=idxf[:, 1:2], in1=sel[:, 0:E],
                                           op0=ALU.is_equal, op1=ALU.add).then_inc(g_step, 1)
            dve.wait_ge(g_step, 4)
            dve.wait_ge(g_exp, 1)
            nc.vector.tensor_tensor_reduce(out=gs, in0=ex, in1=sel[:, E:2 * E], scale=1.0, scalar=0.0,
                                           op0=ALU.mult, op1=ALU.add, accum_out=gsum).then_inc(lg_in, 1)
            dve.wait_ge(lg_in, 3)
            nc.vector.reciprocal(grec, gsum).then_inc(lg_in, 1)
            dve.wait_ge(lg_in, 4)
            nc.vector.tensor_scalar(gs, gs, grec, float(LORA_SCALE), ALU.mult, ALU.mult).then_inc(g_step, 1)
            dve.wait_ge(g_step, 5)
            nc.vector.tensor_tensor(krot[:, 0:E * R].rearrange("p (e r) -> p e r", e=E),
                                    ps[:, E:E + E * R].rearrange("p (e r) -> p e r", e=E),
                                    gs.unsqueeze(2).broadcast_to([P, E, R]), ALU.mult).then_inc(g_step, 1)
            dve.wait_ge(mid_ps, 1)
            nc.vector.tensor_copy(krot[0:E * R, 128:256], ps[0:E * R, UW:UW + P]).then_inc(mid_t, 1)
            for n in range(2):
                dve.wait_ge(delta, n + 1)
                nc.vector.tensor_tensor(blk(soft, n), blk(soft, n), blk(pa, n), ALU.add).then_inc(y_out, 1)


def delayed_sum(nc, dve, gen, st, e8, top8, idx8, corr, q1, py, x2):
    count = [0]

    def done(ins):
        count[0] += 1
        ins.then_inc(gen, 1)
        dve.wait_ge(gen, count[0])

    V = nc.vector
    lag, mult, taken, weight = st[:, 66:74], st[:, 74:82], st[:, 82:90], st[:, 28:36]
    lags, weights, prod = st[:, 36:52], st[:, 52:60], None
    tmp, tau, coef, total = st[:, 90:91], st[:, 91:92], st[:, 92:93], st[:, 93:94]
    n0 = float(HALF // 2 + 1)
    done(V.max_index(idx8[:, :], top8[:, :], corr))
    done(V.tensor_copy(lag, idx8[:, :]))
    done(V.tensor_scalar(mult, lag, n0, None, ALU.is_ge))
    done(V.tensor_scalar(taken, lag, -2.0, float(3 * HALF // 2 + 1), ALU.mult, ALU.add))
    done(V.tensor_tensor(taken, taken, mult, ALU.mult))
    done(V.tensor_tensor(lag, lag, taken, ALU.add))
    done(V.tensor_scalar(mult, lag, 0.0, -1.0, ALU.is_equal, ALU.mult))
    done(V.tensor_scalar(taken, lag, float(HALF), None, ALU.is_equal))
    done(V.tensor_tensor(mult, mult, taken, ALU.subtract))
    done(V.tensor_scalar(mult, mult, 2.0, None, ALU.add))
    done(V.memset(taken[:, 0:1], float(TOPK)))
    for j in range(1, 8):
        done(V.tensor_tensor(taken[:, j:j + 1], taken[:, j - 1:j], mult[:, j - 1:j], ALU.subtract))
    done(V.tensor_scalar(taken, taken, 0.0, None, ALU.max))
    done(V.tensor_tensor(taken, taken, mult, ALU.min))
    done(V.tensor_copy(weight, e8))
    done(V.tensor_tensor(weights, weight, taken, ALU.mult))
    done(V.tensor_reduce(total, weights, mybir.AxisListType.X, ALU.add))
    done(V.reciprocal(tmp, total))
    done(V.tensor_scalar(weight, weight, tmp, None, ALU.mult))
    done(V.tensor_copy(lags[:, 0:8], lag))
    done(V.tensor_scalar(lags[:, 8:16], lag, -1.0, float(D), ALU.mult, ALU.add))
    done(V.scalar_tensor_tensor(out=mult, in0=taken, scalar=2.0, in1=weight, op0=ALU.is_ge, op1=ALU.mult))
    done(V.scalar_tensor_tensor(out=weight, in0=taken, scalar=1.0, in1=weight, op0=ALU.is_ge, op1=ALU.mult))
    done(V.tensor_copy(q1[:, D:2 * D], q1[:, 0:D]))
    done(V.tensor_copy(x2, py[:, :]))
    done(V.memset(tau, 0.0))
    with dve.Fori(0, D) as t:
        n = count[0] + 6 * t
        steps = (
            lambda: V.scalar_tensor_tensor(out=taken, in0=lags[:, 0:8], scalar=tau, in1=weight, op0=ALU.is_equal,
                                           op1=ALU.mult),
            lambda: V.scalar_tensor_tensor(out=weights, in0=lags[:, 8:16], scalar=tau, in1=mult, op0=ALU.is_equal,
                                           op1=ALU.mult),
            lambda: V.tensor_tensor(taken, taken, weights, ALU.add),
            lambda: V.tensor_reduce(coef, taken, mybir.AxisListType.X, ALU.add),
            lambda: V.scalar_tensor_tensor(out=x2, in0=q1[:, bass.ds(t, D)], scalar=coef, in1=x2, op0=ALU.mult,
                                           op1=ALU.add),
            lambda: V.tensor_scalar(tau, tau, 1.0, None, ALU.add),
        )
        for i, step in enumerate(steps):
            step().then_inc(gen, 1)
            dve.wait_ge(gen, n + i + 1)


def tables():
    f32 = np.float32
    half = np.arange(0, DK, 2, dtype=f32) / f32(DK)
    inv = (f32(1.0) / np.power(f32(10000.0), half)).astype(f32)
    ang = np.arange(SK, dtype=f32)[:, None] * inv[None, :]
    cos, sin = np.cos(ang.astype(np.float64)), np.sin(ang.astype(np.float64))
    cos_k = np.concatenate([cos, cos], 1).T.astype(f32)
    sin_k = np.concatenate([sin, -sin], 1).T.astype(f32)
    scale = 1.0 / np.sqrt(float(DK))
    cos_q = np.tile(np.concatenate([cos, cos], 1)[:SQ] * scale, (B, 1)).astype(f32)
    sin_q = np.tile(np.concatenate([-sin, sin], 1)[:SQ] * scale, (B, 1)).astype(f32)
    t = np.arange(HALF)[:, None]

    def angle(f, u):
        return 2 * np.pi * ((f * u) % D) / D

    fe_re, fe_im = np.arange(0, HALF + 1, 2), np.arange(2, HALF, 2)
    fo = np.arange(1, HALF, 2)
    fwd_e = np.concatenate([np.cos(angle(fe_re[None], t)), -np.sin(angle(fe_im[None], t))], 1)
    fwd_o = np.concatenate([np.cos(angle(fo[None], t)), -np.sin(angle(fo[None], t))], 1)
    lag = np.arange(LAGS)[None, :]
    wt = np.where((fe_re == 0) | (fe_re == HALF), 1.0, 2.0)[:, None]
    inv_e = np.concatenate([wt * np.cos(angle(fe_re[:, None], lag)), 2 * np.cos(angle(fe_im[:, None], lag))], 0) / D
    one = 2 * np.cos(angle(fo[:, None], lag)) / D
    one[:, HALF // 2] = 0.0
    inv_o = np.concatenate([one, one], 0)
    tab_f = np.concatenate([fwd_e, fwd_o], 0).reshape(8, P, UW).astype(f32)
    tab_i = np.concatenate([inv_e, inv_o], 0).reshape(4, 2, P, LAGS).transpose(0, 2, 1, 3).reshape(4, P, 2 * LAGS)
    return dict(tab_f=tab_f, tab_i=tab_i.astype(f32), cos_k=cos_k, sin_k=sin_k, cos_q=cos_q, sin_q=sin_q,
                ident=np.eye(P, dtype=f32), iota=np.tile(np.arange(E, dtype=f32), (P, 1)))


def kernel(x, ctx_4096, mask_BxSxS2_ff0, L0_xattn_wq, L0_xattn_wk, L0_xattn_wv, L0_xattn_wo, L0_ffn_A, L0_ffn_B,
           L0_ffn_Wr):
    import concourse.bacc as bacc
    from concourse.bass_utils import run_bass_kernel_spmd

    def wkv_units(w):
        return w.reshape(2, 4, P, HKV, DK).transpose(3, 0, 2, 1, 4).reshape(HKV, 2, P, UW)

    c = tables()
    arrays = {
        "x": x.reshape(T, D),
        "ctx_u": ctx_4096.reshape(B, KB, UW, CH, P).transpose(0, 1, 3, 4, 2).reshape(B, CTX_U, P, UW),
        "mask": mask_BxSxS2_ff0,
        "wkv_u": np.concatenate([wkv_units(np.asarray(L0_xattn_wk)), wkv_units(np.asarray(L0_xattn_wv))], 1),
        "wq_u": np.asarray(L0_xattn_wq).reshape(CH, P, HKV, UW).transpose(2, 0, 1, 3),
        "wo_u": np.asarray(L0_xattn_wo).reshape(HKV, G, P, 2, UW).transpose(0, 1, 3, 2, 4).reshape(HKV, W_U, P, UW),
        "tab_f": c["tab_f"], "tab_i": c["tab_i"], "cos_k": c["cos_k"], "sin_k": c["sin_k"],
        "cos_q": c["cos_q"], "sin_q": c["sin_q"], "ident_d": c["ident"],
        "aw": np.concatenate([np.asarray(L0_ffn_Wr).T, np.asarray(L0_ffn_A).reshape(E * R, D).T], 1)
        .reshape(CH, P, E + E * R).transpose(1, 0, 2).reshape(P, CH * (E + E * R)),
        "bt": np.asarray(L0_ffn_B).transpose(0, 2, 1).reshape(E * R, D),
        "iota_d": c["iota"],
    }
    arrays = {k: np.ascontiguousarray(v) for k, v in arrays.items()}
    nc = bacc.Bacc("TRN2", target_bir_lowering=False, num_devices=1)
    args = {k: nc.dram_tensor(k + "_dram", list(v.shape), mybir.dt.from_np(v.dtype), kind="ExternalInput").ap()
            for k, v in arrays.items()}
    out = nc.dram_tensor("out_dram", [T, D], F32, kind="ExternalOutput").ap()
    perceiver_kernel(nc, out=out, **args)
    r = run_bass_kernel_spmd(nc, [{k + "_dram": v for k, v in arrays.items()}], core_ids=[0])
    return r.results[0]["out_dram"].reshape(B, SQ, D)
```

```python
from contextlib import ExitStack

import numpy as np

import concourse.bass as bass
from concourse import mybir

ALU = mybir.AluOpType
ACT = mybir.ActivationFunctionType
F32 = mybir.dt.float32
F32R = mybir.dt.float32r
I32 = mybir.dt.int32
U32 = mybir.dt.uint32

P = 128
B, SQ, D = 2, 64, 1024
SK = 1024
HQ, HKV, DK = 32, 8, 128
G = HQ // HKV
T = B * SQ
CH = D // P
UW = 512
KB = SK // UW
STEPS = B * HKV
RING = 6
HALF = D // 2
LAGS = HALF // 2 + 2
SLOT = max(UW, 2 * LAGS)
F_COLS, I_COLS = CH * UW, CH * LAGS
E, R = 4, 16
LORA_SCALE = 16.0 / np.sqrt(16.0)
EPS = 1e-5
TOPK = 6
LOWEST = -3.0e38

WK_U, WV_U, W_U, CTX_U = 2, 2, 8, KB * CH
FIRST_WV = WK_U + CTX_U
FIRST_W = FIRST_WV + WV_U
FIRST_WK1 = FIRST_W + W_U
PRO_U = FIRST_WK1 + WK_U
STEP_U = W_U + WV_U + WK_U
CTX1 = PRO_U + STEP_U * (HKV - 1)
STEP7_U = CTX1 + CH
BASE1 = STEP7_U + STEP_U
STEP15_U = BASE1 + STEP_U * (HKV - 1) - WK_U
TAB_U = STEP15_U + W_U
assert STEP_U % RING == 0


def wk0_unit(j):
    return 0 if j == 0 else 5


def ctx0_unit(i):
    return 1 + i if i < 4 else 2 + i


class Step:

    def __init__(self, s, at):
        self.s, self.slope = s, STEP_U
        if at < HKV - 1:
            self.first = PRO_U
        elif at == HKV - 1:
            self.first, self.slope = STEP7_U, 0
        elif at <= STEPS - 2:
            self.first = BASE1 - STEP_U * HKV
        else:
            self.first, self.slope = STEP15_U, 0

    def w(self, j):
        return Unit(self.first + j, self.slope, self.s)

    def wv(self, j):
        return self.w(W_U + j)

    def wk(self, j):
        return self.w(W_U + WV_U + j)


class Unit:

    def __init__(self, static, slope=0, s=0):
        self.static, self.slope, self.s = static, slope, s
        self.slot = static % RING

    def count(self, plus):
        return self.static + plus + (self.slope * self.s if self.slope else 0)

    def arrivals(self):
        return 16 * (self.static // RING + 1) + (16 * (self.slope // RING) * self.s if self.slope else 0)


def perceiver_kernel(nc, x, ctx_u, mask, wkv_u, wq_u, wo_u, tab_f, tab_i, cos_k, sin_k, cos_q, sin_q,
                     ident_d, aw, bt, iota_d, out):
    with ExitStack() as stack:
        def sb(name, cols, dt=F32, rows=P):
            return stack.enter_context(nc.sbuf_tensor(name, [rows, cols], dt))

        def pb(name):
            return stack.enter_context(nc.psum_tensor(name, [P, 2 * UW], F32))

        def sem(name):
            return stack.enter_context(nc.semaphore(name))

        ctx_hi, ctx_lo = sb("ctx_hi", CTX_U * UW, F32R), sb("ctx_lo", CTX_U * UW, F32R)
        wk_hi, wk_lo = sb("wk_hi", CH * P, F32R), sb("wk_lo", CH * P, F32R)
        wv_hi, wv_lo = sb("wv_hi", CH * P, F32R), sb("wv_lo", CH * P, F32R)
        w_hi, w_lo = sb("w_hi", W_U * UW, F32R), sb("w_lo", W_U * UW, F32R)
        raw = sb("raw", RING * SLOT)
        k_hi, k_lo = sb("k_hi", SK, F32R), sb("k_lo", SK, F32R)
        v_hi, v_lo = sb("v_hi", SK, F32R), sb("v_lo", SK, F32R)
        soft = sb("soft", 2 * SK)
        pt_hi, pt_lo = sb("pt_hi", 2 * UW, F32R), sb("pt_lo", 2 * UW, F32R)
        cosk, sink = sb("cosk", SK), sb("sink", SK)
        cosq, sinq = sb("cosq", DK), sb("sinq", DK)
        maskt = sb("maskt", SK)
        q1 = sb("q1", HKV * G * SQ)
        o0 = sb("o0", HKV * G * SQ)
        q_hi, q_lo = sb("q_hi", G * SQ, F32R), sb("q_lo", G * SQ, F32R)
        o_hi, o_lo = sb("o_hi", G * T, F32R), sb("o_lo", G * T, F32R)
        xt_hi, xt_lo = sb("xt_hi", CH * T, F32R), sb("xt_lo", CH * T, F32R)
        krot, kswap = sb("krot", KB * UW), sb("kswap", UW)
        ident = sb("ident", P)
        ones = sb("ones", 2)
        st = sb("st", 112)
        top8 = sb("top8", 8)
        flag_i = sb("flag_i", 2, I32)
        idx8 = sb("idx8", 8, U32)

        mx, nm, rs, ri = st[:, 0:4], st[:, 4:6], st[:, 6:8], st[:, 8:10]
        bn, ag, rstd, nbias = st[:, 10:22], st[:, 22:24], st[:, 24:25], st[:, 25:26]
        gap, near = st[:, 26:27], st[:, 27:28]
        lg, ex, sel, gs = st[:, 28:36], st[:, 36:40], st[:, 40:48], st[:, 48:52]
        idxf, iota4 = st[:, 52:60], st[:, 60:64]
        gate = st[:, 108:112]
        ve, sd, rec, nwt = st[:, 104:105], st[:, 105:106], st[:, 106:107], st[:, 107:108]
        neg0, e8 = st[:, 94:95], st[:, 96:104]
        gsum, grec = st[:, 64:65], st[:, 65:66]

        pk = pb("pk")
        pa = pb("pa")
        ps = pb("ps")
        py = pb("py")

        raw_in = [sem(f"raw_in{i}") for i in range(RING)]
        x_in, tab_in, mask_in, late_in, out_done = (sem(n) for n in ("x_in", "tab_in", "mask_in", "late_in", "out_done"))
        qtab_in = sem("qtab_in")
        unit_hi, unit_lo = sem("unit_hi"), sem("unit_lo")
        ones_set = sem("ones_set")
        ln_bn, ln_ag, ln_var, ln_rstd, ln_out = (sem(n) for n in ("ln_bn", "ln_ag", "ln_var", "ln_rstd", "ln_out"))
        ln_sd = sem("ln_sd")
        xt_ps, xt_h, xt_l, seeded = sem("xt_ps"), sem("xt_h"), sem("xt_l"), sem("seeded")
        kproj, k_mul, k_rot, k_h, k_l = sem("kproj"), sem("k_mul"), sem("k_rot"), sem("k_h"), sem("k_l")
        vproj, vt_raw, vtr, v_h, v_l = sem("vproj"), sem("vt_raw"), sem("vtr"), sem("v_h"), sem("v_l")
        qproj, q_mul, q_rot, qtr, q_h, q_l = (sem(n) for n in ("qproj", "q_mul", "q_rot", "qtr", "q_h", "q_l"))
        scored, masked, nmax, expd, recip, prob = (sem(n) for n in ("scored", "masked", "nmax", "expd", "recip", "prob"))
        ptr, pt_h, pt_l, pv = sem("ptr"), sem("pt_h"), sem("pt_l"), sem("pv")
        o_raw, o_h, o_l, w_used = sem("o_raw"), sem("o_h"), sem("o_l"), sem("w_used")
        fold, ab_ps, ab_h, ab_l, dft = sem("fold"), sem("ab_ps"), sem("ab_h"), sem("ab_l"), sem("dft")
        sq, sq_ps, sq_h, sq_l, idft = sem("sq"), sem("sq_ps"), sem("sq_h"), sem("sq_l"), sem("idft")
        even_out, lagged, topped, gapped, near_ps, flagged = (
            sem(n) for n in ("even_out", "lagged", "topped", "gapped", "near_ps", "flagged"))
        x2_done, h_ps, h_t, lora, lg_in, lg_top, g_exp, g_step, mid_ps, mid_t, delta, y_out = (
            sem(n) for n in ("x2_done", "h_ps", "h_t", "lora", "lg_in", "lg_top", "g_exp", "g_step", "mid_ps",
                             "mid_t", "delta", "y_out"))
        h_t1 = sem("h_t1")
        weighed = sem("weighed")
        gen = sem("gen")

        def raw_ap(u, cols=UW):
            return raw[:, u.slot * SLOT:u.slot * SLOT + cols]

        def blk(t, i, w=UW):
            return t[:, i * w:(i + 1) * w]

        block = stack.enter_context(nc.Block())

        @block.sync
        def _(sp):
            def load_unit(u, src, wait=True, cols=UW):
                if wait:
                    sp.wait_ge(unit_lo, u.count(1 - RING))
                sp.dma_start(raw_ap(u, cols), src).then_inc(raw_in[u.slot], 16)

            def load_pro(n, src):
                load_unit(Unit(n), src, wait=n >= RING)

            def load_wv(step, head):
                for i in range(WV_U):
                    load_unit(step.wv(i), wkv_u[head, WK_U + i])

            def load_wk(step, head):
                for i in range(WK_U):
                    load_unit(step.wk(i), wkv_u[head, i])

            def load_w(step, table, head):
                for j in range(W_U):
                    load_unit(step.w(j), table[head, j])

            def load_mask(b):
                for h in range(2):
                    sp.dma_start(maskt[h * SQ:(h + 1) * SQ, :], mask[b]).then_inc(mask_in, 16)

            load_pro(wk0_unit(0), wkv_u[0, 0])
            for i in range(4):
                load_pro(ctx0_unit(i), ctx_u[0, i])
            load_pro(wk0_unit(1), wkv_u[0, 1])
            for i in range(4, CTX_U):
                load_pro(ctx0_unit(i), ctx_u[0, i])
                if i == 12:
                    sp.dma_start(soft[:, 0:D], x).then_inc(x_in, 16)
                    sp.dma_start(ident[:, :], ident_d).then_inc(x_in, 16)
            for i in range(WV_U):
                load_pro(FIRST_WV + i, wkv_u[0, WK_U + i])
            sp.dma_start(cosk[:, :], cos_k).then_inc(tab_in, 16)
            sp.dma_start(sink[:, :], sin_k).then_inc(tab_in, 16)
            for i in range(W_U):
                load_pro(FIRST_W + i, wq_u[0, i])
            sp.dma_start(cosq[:, :], cos_q).then_inc(qtab_in, 16)
            sp.dma_start(sinq[:, :], sin_q).then_inc(qtab_in, 16)
            load_mask(0)
            for i in range(WK_U):
                load_pro(FIRST_WK1 + i, wkv_u[1, i])

            with sp.Fori(0, HKV - 2) as s:
                step = Step(s, 0)
                load_w(step, wq_u, s + 1)
                load_wv(step, s + 1)
                load_wk(step, s + 2)
            step = Step(HKV - 2, HKV - 2)
            load_w(step, wq_u, HKV - 1)
            load_wv(step, HKV - 1)
            load_wk(step, 0)
            for i in range(CH):
                load_unit(Unit(CTX1 + i), ctx_u[1, i])
            step = Step(HKV - 1, HKV - 1)
            for i in range(CH):
                load_unit(step.w(i), ctx_u[1, CH + i])
            load_wv(step, 0)
            load_wk(step, 1)
            sp.wait_ge(masked, 4 * HKV)
            load_mask(1)
            with sp.Fori(HKV, STEPS - 2) as s:
                step = Step(s, HKV)
                load_w(step, wo_u, s - HKV)
                load_wv(step, s - HKV + 1)
                load_wk(step, s - HKV + 2)
            step = Step(STEPS - 2, STEPS - 2)
            load_w(step, wo_u, HKV - 2)
            load_wv(step, HKV - 1)
            load_w(Step(STEPS - 1, STEPS - 1), wo_u, HKV - 1)
            for i in range(CH):
                load_unit(Unit(TAB_U + i), tab_f[i])
            for i in range(CH // 2):
                load_unit(Unit(TAB_U + CH + i), tab_i[i], cols=2 * LAGS)
            sp.wait_ge(k_rot, KB * STEPS)
            sp.dma_start(cosk[0:E * R, :], bt).then_inc(late_in, 16)
            sp.dma_start(sink[:, 0:CH * (E + E * R)], aw).then_inc(late_in, 16)
            sp.dma_start(iota4, iota_d).then_inc(late_in, 16)
            for i in range(2):
                sp.wait_ge(y_out, i + 1)
                sp.dma_start(out[:, i * UW:(i + 1) * UW], blk(soft, i)).then_inc(out_done, 16)
            sp.wait_ge(out_done, 32)

        @block.tensor
        def _(pe):
            def product(acc, st_hi, st_lo, mv_hi, mv_lo, first, last):
                nc.tensor.matmul(acc, st_lo, mv_hi, start=first, stop=False)
                nc.tensor.matmul(acc, st_hi, mv_lo, start=False, stop=False)
                return nc.tensor.matmul(acc, st_hi, mv_hi, start=False, stop=last)

            def project(acc, hi, lo, b, chunks=range(CH), ctx_at=None):
                for c in chunks:
                    if ctx_at is not None:
                        pe.wait_ge(unit_lo, ctx_at(c) + 1)
                    mm = product(acc, blk(hi, c, P), blk(lo, c, P), blk(ctx_hi, b * CH + c),
                                 blk(ctx_lo, b * CH + c), c == 0, c == CH - 1)
                return mm

            def k_project(m, b, wk_ready=None, chunks=range(CH), ctx_at=None, again=True):
                if wk_ready is not None:
                    pe.wait_ge(unit_lo, wk_ready)
                if again and 0 in chunks:
                    pe.wait_ge(k_rot, KB * m + b - 1)
                mm = project(blk(pk, b), wk_hi, wk_lo, b, chunks, ctx_at)
                if CH - 1 in chunks:
                    mm.then_inc(kproj, 1)

            def v_project(m, b, wv_ready=None, chunks=range(CH), again=True):
                if wv_ready is not None:
                    pe.wait_ge(unit_lo, wv_ready)
                if again:
                    pe.wait_ge(pt_l, 4 * m + b - 1)
                mm = project(blk(pa, b), wv_hi, wv_lo, b, chunks)
                if CH - 1 in chunks:
                    mm.then_inc(vproj, 1)

            def v_transposes(m, b):
                pe.wait_ge(vt_raw, KB * m + b + 1)
                for c in range(4):
                    mm = nc.tensor.transpose(pa[:, b * UW + c * P:b * UW + (c + 1) * P],
                                             soft[:, b * UW + c * P:b * UW + (c + 1) * P], ident[:, :])
                mm.then_inc(vtr, 1)

            def q_project(m, unit_at, again=True):
                if again:
                    pe.wait_ge(masked, 4 * m)
                for c in range(CH):
                    pe.wait_ge(unit_lo, unit_at(c).count(1))
                    mm = product(blk(ps, 1), blk(xt_hi, c, P), blk(xt_lo, c, P), blk(w_hi, c), blk(w_lo, c),
                                 c == 0, c == CH - 1)
                mm.then_inc(qproj, 1)

            def q_transposes(m, again=True):
                pe.wait_ge(q_rot, m + 1)
                if again:
                    pe.wait_ge(o_raw, m)
                for h in range(G):
                    mm = nc.tensor.transpose(blk(ps, h, P), soft[:, SK + h * P:SK + (h + 1) * P], ident[:, :])
                mm.then_inc(qtr, 1)

            def scores(s, o_left=None, pause=None):
                pe.wait_ge(q_l, s + 1)
                if o_left is not None:
                    pe.wait_ge(*o_left)
                for i in range(4):
                    t, b = divmod(i, 2)
                    if t == 0:
                        pe.wait_ge(k_l, KB * s + b + 1)
                    else:
                        pe.wait_ge(masked, 4 * s + i - 1)
                    product(blk(ps, b), blk(q_hi, t, P), blk(q_lo, t, P), blk(k_hi, b), blk(k_lo, b),
                            True, True).then_inc(scored, 1)
                    if i == 0:
                        v_transposes(s, 1)
                    elif i == 1 and pause is not None:
                        pause()

            def turn(s, i):
                if i == 0:
                    pe.wait_ge(prob, 2 * s + 2)
                if i < 2:
                    pe.wait_ge(v_l, KB * s + i + 1)
                else:
                    pe.wait_ge(pt_l, 4 * s + i - 1)
                for c in range(2):
                    for t in range(2):
                        mm = nc.tensor.transpose(
                            pa[:, (i % 2) * UW + c * 256 + t * P:(i % 2) * UW + c * 256 + (t + 1) * P],
                            soft[:, t * SK + (2 * i + c) * P:t * SK + (2 * i + c + 1) * P], ident[:, :])
                mm.then_inc(ptr, 1)

            def weigh(s, i):
                pe.wait_ge(pt_l, 4 * s + i + 1)
                for c in range(2):
                    k, m = 2 * i + c, (i % 2) * UW + c * 256
                    mm = product(ps[:, 0:G * SQ], blk(v_hi, k, P), blk(v_lo, k, P), pt_hi[:, m:m + 256],
                                 pt_lo[:, m:m + 256], k == 0, k == CH - 1)
                mm.then_inc(pv, 1)

            def attend_and_k(s, wk_ready, ctx_at=(None, None)):
                scores(s, pause=lambda: k_project(s + 1, 0, wk_ready, chunks=(0,), ctx_at=ctx_at[0]))
                k_project(s + 1, 0, chunks=range(1, CH), ctx_at=ctx_at[0])
                turn(s, 0)
                turn(s, 1)
                k_project(s + 1, 1, chunks=range(0, CH // 2), ctx_at=ctx_at[1])
                weigh(s, 0)
                turn(s, 2)
                weigh(s, 1)
                turn(s, 3)
                k_project(s + 1, 1, chunks=range(CH // 2, CH), ctx_at=ctx_at[1])
                weigh(s, 2)
                weigh(s, 3)

            def out_project(s, unit_at, final, js=range(W_U)):
                pe.wait_ge(o_l, s - HKV + 1)
                for j in js:
                    h, n = divmod(j, 2)
                    pe.wait_ge(unit_lo, unit_at(j).count(1))
                    mm = product(blk(py, n), blk(o_hi, h, T), blk(o_lo, h, T), blk(w_hi, j), blk(w_lo, j),
                                 False, final and h == G - 1)
                if W_U - 1 in js:
                    mm.then_inc(w_used, 1)

            for b in range(KB):
                k_project(0, b, ctx_at=lambda c, b=b: ctx0_unit(b * CH + c), again=False)
            v_project(0, 0, FIRST_WV + WV_U, again=False)
            pe.wait_ge(x_in, 32)
            for n in range(2):
                mm = nc.tensor.matmul(blk(py, n), ident[:, :], blk(soft, n), start=True, stop=False)
            mm.then_inc(seeded, 1)
            pe.wait_ge(ln_out, 1)
            for n in range(2):
                for c in range(4):
                    mm = nc.tensor.transpose(ps[:, n * UW + c * P:n * UW + (c + 1) * P],
                                             soft[:, D + n * UW + c * P:D + n * UW + (c + 1) * P], ident[:, :])
                mm.then_inc(xt_ps, 1)
            pe.wait_ge(xt_l, 2)
            q_project(0, lambda j: Unit(FIRST_W + j), again=False)
            v_project(0, 1, chunks=range(0, 6), again=False)
            q_transposes(0, again=False)
            v_project(0, 1, chunks=range(6, CH), again=False)
            v_transposes(0, 0)

            def step_0(s, at):
                step = Step(s, at)
                attend_and_k(s, step.w(0).count(0))
                q_project(s + 1, step.w)
                v_project(s + 1, 0, step.wv(1).count(1))
                q_transposes(s + 1)
                v_project(s + 1, 1)
                v_transposes(s + 1, 0)

            with pe.Fori(0, HKV - 2) as s:
                step_0(s, 0)
            step_0(HKV - 2, HKV - 2)
            s = HKV - 1
            step = Step(s, s)
            attend_and_k(s, None, (lambda c: CTX1 + c, lambda c: STEP7_U + c))
            v_project(s + 1, 0, step.wv(1).count(1))
            v_project(s + 1, 1)
            v_transposes(s + 1, 0)

            def step_1(s, at, project_o=True):
                step = Step(s, at)
                attend_and_k(s, step.w(0).count(0))
                v_project(s + 1, 0, step.wv(1).count(1))
                if project_o:
                    out_project(s, step.w, final=False)
                v_project(s + 1, 1)
                v_transposes(s + 1, 0)

            with pe.Fori(HKV, STEPS - 2) as s:
                step_1(s, HKV)
            s = STEPS - 2
            step_1(s, s, project_o=False)
            scores(s + 1, (o_l, HKV - 1))
            out_project(s, Step(s, s).w, final=False, js=range(0, 6))
            turn(s + 1, 0)
            turn(s + 1, 1)
            out_project(s, Step(s, s).w, final=False, js=range(6, W_U))
            s = STEPS - 1
            for i in range(4):
                weigh(s, i)
                if i < 2:
                    turn(s, i + 2)
            out_project(s, Step(s, s).w, final=True)

            def transposes(dst, src, done):
                for n in range(2):
                    for c in range(4):
                        at = n * UW + c * P
                        mm = nc.tensor.transpose(dst[:, at:at + P], src[:, at:at + P], ident[:, :])
                    mm.then_inc(done, 1)

            pe.wait_ge(fold, 2)
            transposes(pk, q1[:, D:2 * D], ab_ps)
            pe.wait_ge(unit_lo, TAB_U + CH)
            for n in range(2):
                pe.wait_ge(ab_l, n + 1)
                for c in range(4):
                    j = 4 * n + c
                    mm = product(blk(pa, n), blk(xt_hi, j, P), blk(xt_lo, j, P), blk(ctx_hi, j), blk(ctx_lo, j),
                                 c == 0, c == 3)
                mm.then_inc(dft, 1)
            pe.wait_ge(sq, 2)
            transposes(pk, o0[:, 0:D], sq_ps)
            pe.wait_ge(unit_lo, TAB_U + CH + CH // 2)
            for n in range(2):
                pe.wait_ge(sq_l, n + 1)
                for c in range(4):
                    j = 4 * n + c
                    at = F_COLS + j * LAGS
                    mm = product(ps[:, n * UW:n * UW + LAGS], blk(k_hi, j, P), blk(k_lo, j, P),
                                 ctx_hi[:, at:at + LAGS], ctx_lo[:, at:at + LAGS], c == 0, c == 3)
                mm.then_inc(idft, 1)
            pe.wait_ge(gapped, 3)
            nc.tensor.matmul(pk[0:1, 0:1], near, ones[:, 0:1], start=True, stop=True).then_inc(near_ps, 1)
            pe.wait_ge(ln_out, 3)
            pe.wait_ge(flagged, 1)
            transposes(pk, soft[:, D:2 * D], h_ps)
            pe.wait_ge(late_in, 48)
            W = E + E * R
            for c in range(CH):
                if c % 4 == 0:
                    pe.wait_ge((h_t, h_t1)[c // 4], 1)
                mm = nc.tensor.matmul(ps[:, 0:W], blk(maskt, c, P), sink[:, c * W:(c + 1) * W],
                                      start=c == 0, stop=c == CH - 1)
            mm.then_inc(lora, 1)
            pe.wait_ge(g_step, 6)
            nc.tensor.transpose(ps[0:E * R, UW:UW + P], krot[:, 0:E * R], ident[:, :]).then_inc(mid_ps, 1)
            pe.wait_ge(mid_t, 1)
            for n in range(2):
                nc.tensor.matmul(blk(pa, n), krot[0:E * R, 128:256], cosk[0:E * R, n * UW:(n + 1) * UW],
                                 start=True, stop=True).then_inc(delta, 1)

        @block.scalar
        def _(act):
            def unit(u, dst, free=None, cols=UW):
                if free is not None:
                    act.wait_ge(*free)
                act.wait_ge(raw_in[u.slot], u.arrivals())
                nc.scalar.copy(dst, raw_ap(u, cols)).then_inc(unit_hi, 1)

            def root(n):
                act.wait_ge(ln_var, n)
                nc.scalar.activation(sd, ve, ACT.Sqrt).then_inc(ln_sd, 1)

            def k_his(m, again=True):
                for b in range(KB):
                    act.wait_ge(k_rot, KB * m + b + 1)
                    if again:
                        act.wait_ge(scored, 4 * m)
                    nc.scalar.copy(blk(k_hi, b), blk(krot, b)).then_inc(k_h, 1)

            def vt_copy(m, b):
                act.wait_ge(vproj, KB * m + b + 1)
                nc.scalar.copy(blk(soft, b), blk(pa, b)).then_inc(vt_raw, 1)

            def v_his(m, again=True):
                for b in range(KB):
                    act.wait_ge(vtr, KB * m + b + 1)
                    if again:
                        act.wait_ge(pv, 4 * m)
                    nc.scalar.copy(blk(v_hi, b), blk(pa, b)).then_inc(v_h, 1)

            def q_his_0(m, again=True):
                act.wait_ge(qtr, m + 1)
                if again:
                    act.wait_ge(scored, 4 * m)
                src = blk(ps, 0).rearrange("p (h b t) -> p b h t", h=G, b=B)
                nc.scalar.copy(q_hi.rearrange("p (h t) -> p h t", h=G), src[:, 0]).then_inc(q_h, 1)
                nc.scalar.copy(q1[:, bass.ds(m * (G * SQ), G * SQ)].rearrange("p (h t) -> p h t", h=G),
                               src[:, 1]).then_inc(q_h, 1)

            def q_his_1(m):
                act.wait_ge(scored, 4 * m)
                nc.scalar.copy(q_hi[:, :], q1[:, bass.ds((m - HKV) * (G * SQ), G * SQ)]).then_inc(q_h, 2)

            def softmax_exp(s):
                for t in range(2):
                    act.wait_ge(nmax, 2 * s + t + 1)
                    nc.scalar.activation(blk(soft, t, SK), blk(soft, t, SK), ACT.Exp, bias=nm[:, t:t + 1],
                                         scale=1.0, accum_out=rs[:, t:t + 1]).then_inc(expd, 1)

            def pt_his(s, turns, first=False):
                for i in turns:
                    act.wait_ge(ptr, 4 * s + i + 1)
                    if i >= 2 or not first:
                        act.wait_ge(pv, 4 * s + i - 1)
                    nc.scalar.copy(blk(pt_hi, i % 2), blk(pa, i % 2)).then_inc(pt_h, 1)

            def keep_o(s):
                act.wait_ge(pv, 4 * s + 4)
                nc.scalar.copy(o0[:, bass.ds(s * (G * SQ), G * SQ)], ps[:, 0:G * SQ]).then_inc(o_raw, 1)

            oh = o_hi.rearrange("p (h b t) -> p b h t", h=G, b=B)

            def o_hi_0(s, first=False):
                if not first:
                    act.wait_ge(w_used, s - HKV)
                nc.scalar.copy(oh[:, 0], o0[:, bass.ds((s - HKV) * (G * SQ), G * SQ)]
                               .rearrange("p (h t) -> p h t", h=G)).then_inc(o_h, 1)

            def o_hi_1(s):
                act.wait_ge(pv, 4 * s + 4)
                nc.scalar.copy(oh[:, 1], ps[:, 0:G * SQ].rearrange("p (h t) -> p h t", h=G)).then_inc(o_h, 1)

            def w_units(units, dst, free):
                for j, (u, at) in enumerate(units):
                    unit(u, blk(dst, at), free if j == 0 else None)

            unit(Unit(wk0_unit(0)), blk(wk_hi, 0))
            for j in range(4):
                unit(Unit(ctx0_unit(j)), blk(ctx_hi, j))
            unit(Unit(wk0_unit(1)), blk(wk_hi, 1))
            for j in range(4, CTX_U):
                unit(Unit(ctx0_unit(j)), blk(ctx_hi, j))
            for j in range(WV_U):
                unit(Unit(FIRST_WV + j), blk(wv_hi, j))
            root(1)
            for j in range(4):
                unit(Unit(FIRST_W + j), blk(w_hi, j))
            for n in range(2):
                act.wait_ge(xt_ps, n + 1)
                nc.scalar.copy(blk(xt_hi, n), blk(ps, n)).then_inc(xt_h, 1)
            for j in range(4, W_U):
                unit(Unit(FIRST_W + j), blk(w_hi, j))
            k_his(0, again=False)
            act.wait_ge(seeded, 1)
            act.wait_ge(ln_out, 1)
            vt_copy(0, 0)
            q_his_0(0, again=False)
            vt_copy(0, 1)
            for j in range(WK_U):
                unit(Unit(FIRST_WK1 + j), blk(wk_hi, j), (kproj, KB))

            def step_act(s, at, batch, w_free, first=False):
                step = Step(s, at)
                w_dst, w_at = (ctx_hi, CH) if at == HKV - 1 else (w_hi, 0)
                v_his(s, again=at > 0)
                softmax_exp(s)
                if at == STEPS - 1:
                    pt_his(s, (0, 1))
                    o_hi_0(s)
                    w_units([(step.w(0), 0)], w_hi, w_free)
                    pt_his(s, (2,))
                    w_units([(step.w(1), 1)], w_hi, None)
                    pt_his(s, (3,))
                    w_units([(step.w(j), j) for j in range(2, 4)], w_hi, None)
                    o_hi_1(s)
                    w_units([(step.w(j), j) for j in range(4, W_U)], w_hi, None)
                    return
                if batch == 1:
                    o_hi_0(s, first)
                w_units([(step.w(j), w_at + j) for j in range(4)], w_dst, w_free)
                pt_his(s, (0, 1), first=at == 0)
                w_units([(step.w(j), w_at + j) for j in range(4, W_U)], w_dst, None)
                w_units([(step.wv(j), j) for j in range(WV_U)], wv_hi, (vproj, KB * (s + 1)))
                pt_his(s, (2, 3))
                if batch == 0:
                    keep_o(s)
                else:
                    o_hi_1(s)
                k_his(s + 1)
                if at < STEPS - 2:
                    w_units([(step.wk(j), j) for j in range(WK_U)], wk_hi, (kproj, KB * (s + 2)))
                vt_copy(s + 1, 0)
                if at < HKV - 1:
                    q_his_0(s + 1)
                else:
                    if at == HKV - 1:
                        act.wait_ge(q_h, 2 * HKV)
                    q_his_1(s + 1)
                if at == HKV - 2:
                    w_units([(Unit(CTX1 + j), j) for j in range(CH)], ctx_hi, (vproj, KB * (s + 1) + 1))
                vt_copy(s + 1, 1)

            step_act(0, 0, 0, (qproj, 1))
            with act.Fori(1, HKV - 2) as s:
                step_act(s, 1, 0, (qproj, s + 1))
            step_act(HKV - 2, HKV - 2, 0, (qproj, HKV - 1))
            step_act(HKV - 1, HKV - 1, 0, (vproj, KB * HKV))
            step_act(HKV, HKV, 1, (qproj, HKV), True)
            with act.Fori(HKV + 1, STEPS - 2) as s:
                step_act(s, HKV + 1, 1, (w_used, s - HKV))
            step_act(STEPS - 2, STEPS - 2, 1, (w_used, HKV - 2))
            step_act(STEPS - 1, STEPS - 1, 1, (w_used, HKV - 1))

            for j in range(CH):
                unit(Unit(TAB_U + j), blk(ctx_hi, j))

            root(2)
            for n in range(2):
                act.wait_ge(ab_ps, n + 1)
                nc.scalar.copy(blk(xt_hi, n), blk(pk, n)).then_inc(ab_h, 1)
            for j in range(CH // 2):
                unit(Unit(TAB_U + CH + j), blk(ctx_hi[:, F_COLS:], j, 2 * LAGS), cols=2 * LAGS)
            for n in range(2):
                act.wait_ge(dft, n + 1)
                nc.scalar.activation(blk(o0, n), blk(pa, n), ACT.Square).then_inc(sq, 1)
            for n in range(2):
                act.wait_ge(sq_ps, n + 1)
                nc.scalar.copy(blk(k_hi, n), blk(pk, n)).then_inc(sq_h, 1)
            act.wait_ge(idft, 1)
            nc.scalar.copy(krot[:, 0:LAGS], ps[:, 0:LAGS]).then_inc(even_out, 1)
            act.wait_ge(gapped, 1)
            nc.scalar.activation(e8, top8[:, :], ACT.Exp, bias=neg0, scale=1.0).then_inc(weighed, 1)
            root(3)
            act.wait_ge(h_ps, 1)
            nc.scalar.copy(blk(maskt, 0), blk(pk, 0)).then_inc(h_t, 1)
            act.wait_ge(lg_top, 1)
            nc.scalar.activation(ex, lg[:, 0:E], ACT.Exp, bias=gap, scale=1.0).then_inc(g_exp, 1)

        @block.vector
        def _(dve):
            def unit(u, hi, lo, at, first=0, cols=UW):
                dve.wait_ge(unit_hi, u.count(1))
                nc.vector.tensor_tensor(blk(lo[:, first:], at, cols), raw_ap(u, cols), blk(hi[:, first:], at, cols),
                                        ALU.subtract).then_inc(unit_lo, 1)

            def lo(dst_lo, src, hi, done, ready=None):
                if ready is not None:
                    dve.wait_ge(*ready)
                nc.vector.tensor_tensor(dst_lo, src, hi, ALU.subtract).then_inc(done, 1)

            def layer_norm(src, dst, n):
                for h in range(2):
                    nc.vector.bn_stats(bn[:, 6 * h:6 * h + 6], blk(src, h)).then_inc(ln_bn, 1)
                dve.wait_ge(ln_bn, 2 * n)
                nc.vector.bn_aggr(ag, bn).then_inc(ln_ag, 1)
                dve.wait_ge(ln_ag, n)
                nc.vector.tensor_scalar(ve, ag[:, 1:2], EPS, None, ALU.add).then_inc(ln_var, 1)
                dve.wait_ge(ln_sd, n)
                nc.vector.reciprocal(rec, sd).then_inc(ln_rstd, 1)
                dve.wait_ge(ln_rstd, 4 * n - 3)
                nc.vector.scalar_tensor_tensor(out=nwt, in0=rec, scalar=rec, in1=ve, op0=ALU.mult,
                                               op1=ALU.mult).then_inc(ln_rstd, 1)
                dve.wait_ge(ln_rstd, 4 * n - 2)
                nc.vector.tensor_scalar(nwt, nwt, -0.5, 1.5, ALU.mult, ALU.add).then_inc(ln_rstd, 1)
                dve.wait_ge(ln_rstd, 4 * n - 1)
                nc.vector.tensor_tensor(rstd, rec, nwt, ALU.mult).then_inc(ln_rstd, 1)
                dve.wait_ge(ln_rstd, 4 * n)
                nc.vector.tensor_scalar(dst, src, ag[:, 0:1], rstd, ALU.subtract, ALU.mult).then_inc(ln_out, 1)

            def rotate(m, b, again=True):
                dve.wait_ge(kproj, KB * m + b + 1)
                src, cs, sn = blk(pk, b), blk(cosk, b), blk(sink, b)
                nc.vector.tensor_tensor(blk(krot, b), src, cs, ALU.mult).then_inc(k_mul, 1)
                if again:
                    dve.wait_ge(k_rot, KB * m + b)
                nc.vector.tensor_tensor(kswap[0:64, :], src[64:128, :], sn[64:128, :], ALU.mult).then_inc(k_mul, 1)
                nc.vector.tensor_tensor(kswap[64:128, :], src[0:64, :], sn[0:64, :], ALU.mult).then_inc(k_mul, 1)
                dve.wait_ge(k_mul, 3 * (KB * m + b + 1))
                nc.vector.tensor_tensor(blk(krot, b), blk(krot, b), kswap[:, :], ALU.add).then_inc(k_rot, 1)

            def k_los(m):
                for b in range(KB):
                    lo(blk(k_lo, b), blk(krot, b), blk(k_hi, b), k_l, (k_h, KB * m + b + 1))

            def v_los(m):
                for b in range(KB):
                    lo(blk(v_lo, b), blk(pa, b), blk(v_hi, b), v_l, (v_h, KB * m + b + 1))

            def rotate_q(m):
                dve.wait_ge(qproj, m + 1)
                q = blk(ps, 1).rearrange("p (h two d) -> p h two d", h=G, two=2)
                cos = cosq[:, :].unsqueeze(1).broadcast_to([P, G, DK])
                sin = sinq[:, :].rearrange("p (two d) -> p two d", two=2).unsqueeze(1).broadcast_to([P, G, 2, DK // 2])
                prod = blk(soft, 2)
                swap = blk(soft, 3).rearrange("p (h two d) -> p h two d", h=G, two=2)
                nc.vector.tensor_tensor(prod.rearrange("p (h d) -> p h d", h=G),
                                        blk(ps, 1).rearrange("p (h d) -> p h d", h=G), cos, ALU.mult).then_inc(q_mul, 1)
                for i in range(2):
                    nc.vector.tensor_tensor(swap[:, :, i, :], q[:, :, 1 - i, :], sin[:, :, i, :],
                                            ALU.mult).then_inc(q_mul, 1)
                dve.wait_ge(q_mul, 3 * m + 3)
                nc.vector.tensor_tensor(prod, prod, blk(soft, 3), ALU.add).then_inc(q_rot, 1)

            def q_lo_0(m):
                lo(q_lo.rearrange("p (h t) -> p h t", h=G),
                   blk(ps, 0).rearrange("p (h b t) -> p b h t", h=G, b=B)[:, 0],
                   q_hi.rearrange("p (h t) -> p h t", h=G), q_l, (q_h, 2 * m + 2))

            def q_lo_1(m):
                lo(q_lo[:, :], q1[:, bass.ds((m - HKV) * (G * SQ), G * SQ)], q_hi[:, :], q_l, (q_h, 2 * m + 2))

            def softmax(s, batch):
                for i in range(4):
                    if i < 2:
                        dve.wait_ge(vtr, KB * s + i + 1)
                    elif i == 2 and batch == 0:
                        dve.wait_ge(qtr, s + 1)
                    dve.wait_ge(scored, 4 * s + i + 1)
                    nc.vector.memset(gate[:, i:i + 1], 0.0)
                    dve.wait_ge(mask_in, 32 * (batch + 1))
                    nc.vector.tensor_tensor_reduce(
                        out=blk(soft, i), in0=blk(ps, i % 2), in1=blk(maskt, i % 2), scale=1.0, scalar=LOWEST,
                        op0=ALU.add, op1=ALU.max, accum_out=mx[:, i:i + 1]).then_inc(masked, 1)
                    if i % 2:
                        t = i // 2
                        dve.wait_ge(masked, 4 * s + i + 1)
                        nc.vector.tensor_scalar(nm[:, t:t + 1], mx[:, i - 1:i], mx[:, i:i + 1], -1.0,
                                                ALU.max, ALU.mult).then_inc(nmax, 1)

            def divide(s):
                for t in range(2):
                    dve.wait_ge(expd, 2 * s + t + 1)
                    nc.vector.reciprocal(ri[:, t:t + 1], rs[:, t:t + 1]).then_inc(recip, 1)
                    dve.wait_ge(recip, 2 * s + t + 1)
                    nc.vector.tensor_scalar(blk(soft, t, SK), blk(soft, t, SK), ri[:, t:t + 1], None,
                                            ALU.mult).then_inc(prob, 1)

            def pt_los(s, turns):
                for i in turns:
                    lo(blk(pt_lo, i % 2), blk(pa, i % 2), blk(pt_hi, i % 2), pt_l, (pt_h, 4 * s + i + 1))

            ol, oh = (t.rearrange("p (h b t) -> p b h t", h=G, b=B) for t in (o_lo, o_hi))

            def o_lo_0(s):
                dve.wait_ge(o_h, 2 * (s - HKV) + 1)
                nc.vector.tensor_tensor(ol[:, 0], o0[:, bass.ds((s - HKV) * (G * SQ), G * SQ)]
                                        .rearrange("p (h t) -> p h t", h=G), oh[:, 0], ALU.subtract)

            def o_lo_1(s):
                lo(ol[:, 1], ps[:, 0:G * SQ].rearrange("p (h t) -> p h t", h=G), oh[:, 1], o_l,
                   (o_h, 2 * (s - HKV) + 2))

            nc.vector.memset(ones[:, :], 1.0).then_inc(ones_set, 1)
            unit(Unit(wk0_unit(0)), wk_hi, wk_lo, 0)
            for j in range(4):
                unit(Unit(ctx0_unit(j)), ctx_hi, ctx_lo, j)
            unit(Unit(wk0_unit(1)), wk_hi, wk_lo, 1)
            for j in range(4, CTX_U):
                unit(Unit(ctx0_unit(j)), ctx_hi, ctx_lo, j)
            for j in range(WV_U):
                unit(Unit(FIRST_WV + j), wv_hi, wv_lo, j)
            dve.wait_ge(x_in, 32)
            layer_norm(soft[:, 0:D], soft[:, D:2 * D], 1)
            for j in range(4):
                unit(Unit(FIRST_W + j), w_hi, w_lo, j)
            dve.wait_ge(tab_in, 32)
            rotate(0, 0, again=False)
            for n in range(2):
                lo(blk(xt_lo, n), blk(ps, n), blk(xt_hi, n), xt_l, (xt_h, n + 1))
            for j in range(4, W_U):
                unit(Unit(FIRST_W + j), w_hi, w_lo, j)
            rotate(0, 1)
            k_los(0)
            dve.wait_ge(qtab_in, 32)
            rotate_q(0)
            q_lo_0(0)
            for j in range(WK_U):
                unit(Unit(FIRST_WK1 + j), wk_hi, wk_lo, j)

            def step_dve(s, at, batch):
                step = Step(s, at)
                w_dst, w_at = ((ctx_hi, ctx_lo), CH) if at == HKV - 1 else ((w_hi, w_lo), 0)
                softmax(s, batch)
                v_los(s)
                divide(s)
                if at == STEPS - 1:
                    pt_los(s, (0, 1))
                    o_lo_0(s)
                    unit(step.w(0), w_hi, w_lo, 0)
                    pt_los(s, (2,))
                    unit(step.w(1), w_hi, w_lo, 1)
                    pt_los(s, (3,))
                    for j in range(2, 4):
                        unit(step.w(j), w_hi, w_lo, j)
                    o_lo_1(s)
                    for j in range(4, W_U):
                        unit(step.w(j), w_hi, w_lo, j)
                    return
                if batch == 1:
                    o_lo_0(s)
                for j in range(4):
                    unit(step.w(j), *w_dst, w_at + j)
                pt_los(s, (0, 1))
                for j in range(4, W_U):
                    unit(step.w(j), *w_dst, w_at + j)
                for j in range(WV_U):
                    unit(step.wv(j), wv_hi, wv_lo, j)
                pt_los(s, (2, 3))
                if batch == 1:
                    o_lo_1(s)
                for b in range(KB):
                    rotate(s + 1, b)
                k_los(s + 1)
                if at < STEPS - 2:
                    for j in range(WK_U):
                        unit(step.wk(j), wk_hi, wk_lo, j)
                if at < HKV - 1:
                    rotate_q(s + 1)
                    q_lo_0(s + 1)
                else:
                    q_lo_1(s + 1)
                if at == HKV - 2:
                    for j in range(CH):
                        unit(Unit(CTX1 + j), ctx_hi, ctx_lo, j)

            with dve.Fori(0, HKV - 2) as s:
                step_dve(s, 0, 0)
            step_dve(HKV - 2, HKV - 2, 0)
            step_dve(HKV - 1, HKV - 1, 0)
            with dve.Fori(HKV, STEPS - 2) as s:
                step_dve(s, HKV, 1)
            step_dve(STEPS - 2, STEPS - 2, 1)
            step_dve(STEPS - 1, STEPS - 1, 1)

            for j in range(CH):
                unit(Unit(TAB_U + j), ctx_hi, ctx_lo, j)

            xn, ab = q1[:, 0:D], q1[:, D:2 * D]
            dve.wait_ge(w_used, HKV)
            layer_norm(py[:, :], xn, 2)
            dve.wait_ge(ln_out, 2)
            nc.vector.tensor_tensor(blk(ab, 0), blk(xn, 0), blk(xn, 1), ALU.add).then_inc(fold, 1)
            nc.vector.tensor_tensor(blk(ab, 1), blk(xn, 0), blk(xn, 1), ALU.subtract).then_inc(fold, 1)
            for n in range(2):
                lo(blk(xt_lo, n), blk(pk, n), blk(xt_hi, n), ab_l, (ab_h, n + 1))
            for j in range(CH // 2):
                unit(Unit(TAB_U + CH + j), ctx_hi, ctx_lo, j, first=F_COLS, cols=2 * LAGS)
            for n in range(2):
                lo(blk(k_lo, n), blk(pk, n), blk(k_hi, n), sq_l, (sq_h, n + 1))
            L0 = HALF // 2 + 1
            corr = o0[:, D:D + HALF + 1]
            dve.wait_ge(idft, 2)
            dve.wait_ge(even_out, 1)
            nc.vector.tensor_tensor(corr[:, 0:L0], krot[:, 0:L0], ps[:, UW:UW + L0], ALU.add).then_inc(lagged, 1)
            nc.vector.tensor_tensor(corr[:, L0:HALF + 1], krot[:, 0:L0 - 1], ps[:, UW:UW + L0 - 1],
                                    ALU.subtract).then_inc(lagged, 1)
            dve.wait_ge(lagged, 2)
            nc.vector.max(top8[:, :], corr).then_inc(topped, 1)
            dve.wait_ge(topped, 1)
            nc.vector.tensor_scalar(neg0, top8[:, 0:1], -1.0, None, ALU.mult).then_inc(gapped, 1)
            nc.vector.tensor_scalar(gap, top8[:, 1:2], top8[:, 0:1], None, ALU.subtract).then_inc(gapped, 1)
            dve.wait_ge(gapped, 2)
            nc.vector.tensor_scalar(near, gap, -110.0, None, ALU.is_ge).then_inc(gapped, 1)
            x2 = soft[:, 0:D]
            nc.vector.tensor_tensor(x2, py[:, :], xn, ALU.add).then_inc(x2_done, 1)
            dve.wait_ge(near_ps, 1)
            nc.vector.tensor_copy(flag_i[0:1, 0:1], pk[0:1, 0:1]).then_inc(flagged, 1)
            dve.wait_ge(flagged, 1)
            dve.wait_ge(x2_done, 1)
            rows_near = dve.value_load(flag_i[0:1, 0:1], min_val=0, max_val=P)
            with dve.If(rows_near > 0):
                dve.wait_ge(weighed, 1)
                delayed_sum(nc, dve, gen, st, e8, top8, idx8, corr, q1, py, x2)
            layer_norm(x2, soft[:, D:2 * D], 3)

            dve.wait_ge(h_ps, 2)
            nc.vector.tensor_copy(blk(maskt, 1), blk(pk, 1)).then_inc(h_t1, 1)
            nc.vector.memset(lg, LOWEST).then_inc(lg_in, 1)
            dve.wait_ge(lg_in, 1)
            dve.wait_ge(lora, 1)
            nc.vector.tensor_copy(lg[:, 0:E], ps[:, 0:E]).then_inc(lg_in, 1)
            dve.wait_ge(lg_in, 2)
            dve.wait_ge(weighed, 1)
            nc.vector.max(top8[:, :], lg).then_inc(topped, 1)
            dve.wait_ge(topped, 2)
            nc.vector.tensor_scalar(gap, top8[:, 0:1], -1.0, None, ALU.mult).then_inc(lg_top, 1)
            nc.vector.max_index(idx8[:, :], top8[:, :], lg).then_inc(g_step, 1)
            dve.wait_ge(g_step, 1)
            nc.vector.tensor_copy(idxf, idx8[:, :]).then_inc(g_step, 1)
            dve.wait_ge(g_step, 2)
            dve.wait_ge(late_in, 48)
            nc.vector.tensor_scalar(sel[:, 0:E], iota4, idxf[:, 0:1], None, ALU.is_equal).then_inc(g_step, 1)
            dve.wait_ge(g_step, 3)
            nc.vector.scalar_tensor_tensor(out=sel[:, E:2 * E], in0=iota4, scalar=idxf[:, 1:2], in1=sel[:, 0:E],
                                           op0=ALU.is_equal, op1=ALU.add).then_inc(g_step, 1)
            dve.wait_ge(g_step, 4)
            dve.wait_ge(g_exp, 1)
            nc.vector.tensor_tensor_reduce(out=gs, in0=ex, in1=sel[:, E:2 * E], scale=1.0, scalar=0.0,
                                           op0=ALU.mult, op1=ALU.add, accum_out=gsum).then_inc(lg_in, 1)
            dve.wait_ge(lg_in, 3)
            nc.vector.reciprocal(grec, gsum).then_inc(lg_in, 1)
            dve.wait_ge(lg_in, 4)
            nc.vector.tensor_scalar(gs, gs, grec, float(LORA_SCALE), ALU.mult, ALU.mult).then_inc(g_step, 1)
            dve.wait_ge(g_step, 5)
            nc.vector.tensor_tensor(krot[:, 0:E * R].rearrange("p (e r) -> p e r", e=E),
                                    ps[:, E:E + E * R].rearrange("p (e r) -> p e r", e=E),
                                    gs.unsqueeze(2).broadcast_to([P, E, R]), ALU.mult).then_inc(g_step, 1)
            dve.wait_ge(mid_ps, 1)
            nc.vector.tensor_copy(krot[0:E * R, 128:256], ps[0:E * R, UW:UW + P]).then_inc(mid_t, 1)
            for n in range(2):
                dve.wait_ge(delta, n + 1)
                nc.vector.tensor_tensor(blk(soft, n), blk(soft, n), blk(pa, n), ALU.add).then_inc(y_out, 1)


def delayed_sum(nc, dve, gen, st, e8, top8, idx8, corr, q1, py, x2):
    count = [0]

    def done(ins):
        count[0] += 1
        ins.then_inc(gen, 1)
        dve.wait_ge(gen, count[0])

    V = nc.vector
    lag, mult, taken, weight = st[:, 66:74], st[:, 74:82], st[:, 82:90], st[:, 28:36]
    lags, weights, prod = st[:, 36:52], st[:, 52:60], None
    tmp, tau, coef, total = st[:, 90:91], st[:, 91:92], st[:, 92:93], st[:, 93:94]
    n0 = float(HALF // 2 + 1)
    done(V.max_index(idx8[:, :], top8[:, :], corr))
    done(V.tensor_copy(lag, idx8[:, :]))
    done(V.tensor_scalar(mult, lag, n0, None, ALU.is_ge))
    done(V.tensor_scalar(taken, lag, -2.0, float(3 * HALF // 2 + 1), ALU.mult, ALU.add))
    done(V.tensor_tensor(taken, taken, mult, ALU.mult))
    done(V.tensor_tensor(lag, lag, taken, ALU.add))
    done(V.tensor_scalar(mult, lag, 0.0, -1.0, ALU.is_equal, ALU.mult))
    done(V.tensor_scalar(taken, lag, float(HALF), None, ALU.is_equal))
    done(V.tensor_tensor(mult, mult, taken, ALU.subtract))
    done(V.tensor_scalar(mult, mult, 2.0, None, ALU.add))
    done(V.memset(taken[:, 0:1], float(TOPK)))
    for j in range(1, 8):
        done(V.tensor_tensor(taken[:, j:j + 1], taken[:, j - 1:j], mult[:, j - 1:j], ALU.subtract))
    done(V.tensor_scalar(taken, taken, 0.0, None, ALU.max))
    done(V.tensor_tensor(taken, taken, mult, ALU.min))
    done(V.tensor_copy(weight, e8))
    done(V.tensor_tensor(weights, weight, taken, ALU.mult))
    done(V.tensor_reduce(total, weights, mybir.AxisListType.X, ALU.add))
    done(V.reciprocal(tmp, total))
    done(V.tensor_scalar(weight, weight, tmp, None, ALU.mult))
    done(V.tensor_copy(lags[:, 0:8], lag))
    done(V.tensor_scalar(lags[:, 8:16], lag, -1.0, float(D), ALU.mult, ALU.add))
    done(V.scalar_tensor_tensor(out=mult, in0=taken, scalar=2.0, in1=weight, op0=ALU.is_ge, op1=ALU.mult))
    done(V.scalar_tensor_tensor(out=weight, in0=taken, scalar=1.0, in1=weight, op0=ALU.is_ge, op1=ALU.mult))
    done(V.tensor_copy(q1[:, D:2 * D], q1[:, 0:D]))
    done(V.tensor_copy(x2, py[:, :]))
    done(V.memset(tau, 0.0))
    with dve.Fori(0, D) as t:
        n = count[0] + 6 * t
        steps = (
            lambda: V.scalar_tensor_tensor(out=taken, in0=lags[:, 0:8], scalar=tau, in1=weight, op0=ALU.is_equal,
                                           op1=ALU.mult),
            lambda: V.scalar_tensor_tensor(out=weights, in0=lags[:, 8:16], scalar=tau, in1=mult, op0=ALU.is_equal,
                                           op1=ALU.mult),
            lambda: V.tensor_tensor(taken, taken, weights, ALU.add),
            lambda: V.tensor_reduce(coef, taken, mybir.AxisListType.X, ALU.add),
            lambda: V.scalar_tensor_tensor(out=x2, in0=q1[:, bass.ds(t, D)], scalar=coef, in1=x2, op0=ALU.mult,
                                           op1=ALU.add),
            lambda: V.tensor_scalar(tau, tau, 1.0, None, ALU.add),
        )
        for i, step in enumerate(steps):
            step().then_inc(gen, 1)
            dve.wait_ge(gen, n + i + 1)


def tables():
    f32 = np.float32
    half = np.arange(0, DK, 2, dtype=f32) / f32(DK)
    inv = (f32(1.0) / np.power(f32(10000.0), half)).astype(f32)
    ang = np.arange(SK, dtype=f32)[:, None] * inv[None, :]
    cos, sin = np.cos(ang.astype(np.float64)), np.sin(ang.astype(np.float64))
    cos_k = np.concatenate([cos, cos], 1).T.astype(f32)
    sin_k = np.concatenate([sin, -sin], 1).T.astype(f32)
    scale = 1.0 / np.sqrt(float(DK))
    cos_q = np.tile(np.concatenate([cos, cos], 1)[:SQ] * scale, (B, 1)).astype(f32)
    sin_q = np.tile(np.concatenate([-sin, sin], 1)[:SQ] * scale, (B, 1)).astype(f32)
    t = np.arange(HALF)[:, None]

    def angle(f, u):
        return 2 * np.pi * ((f * u) % D) / D

    fe_re, fe_im = np.arange(0, HALF + 1, 2), np.arange(2, HALF, 2)
    fo = np.arange(1, HALF, 2)
    fwd_e = np.concatenate([np.cos(angle(fe_re[None], t)), -np.sin(angle(fe_im[None], t))], 1)
    fwd_o = np.concatenate([np.cos(angle(fo[None], t)), -np.sin(angle(fo[None], t))], 1)
    lag = np.arange(LAGS)[None, :]
    wt = np.where((fe_re == 0) | (fe_re == HALF), 1.0, 2.0)[:, None]
    inv_e = np.concatenate([wt * np.cos(angle(fe_re[:, None], lag)), 2 * np.cos(angle(fe_im[:, None], lag))], 0) / D
    one = 2 * np.cos(angle(fo[:, None], lag)) / D
    one[:, HALF // 2] = 0.0
    inv_o = np.concatenate([one, one], 0)

    tab_f = np.concatenate([fwd_e, fwd_o], 0).reshape(CH, P, UW).astype(f32)
    tab_i = np.concatenate([inv_e, inv_o], 0).astype(f32)
    tab_i = tab_i.reshape(CH // 2, 2, P, LAGS).transpose(0, 2, 1, 3).reshape(CH // 2, P, 2 * LAGS)
    return dict(tab_f=tab_f, tab_i=tab_i, cos_k=cos_k, sin_k=sin_k, cos_q=cos_q, sin_q=sin_q,
                ident=np.eye(P, dtype=f32), iota=np.tile(np.arange(E, dtype=f32), (P, 1)))


def kernel(x, ctx_4096, mask_BxSxS2_ff0, L0_xattn_wq, L0_xattn_wk, L0_xattn_wv, L0_xattn_wo, L0_ffn_A, L0_ffn_B,
           L0_ffn_Wr):
    import concourse.bacc as bacc
    from concourse.bass_utils import run_bass_kernel_spmd

    def wkv_units(w):
        return w.reshape(2, 4, P, HKV, DK).transpose(3, 0, 2, 1, 4).reshape(HKV, 2, P, UW)

    c = tables()
    arrays = {
        "x": x.reshape(T, D),
        "ctx_u": ctx_4096.reshape(B, KB, UW, CH, P).transpose(0, 1, 3, 4, 2).reshape(B, CTX_U, P, UW),
        "mask": mask_BxSxS2_ff0,
        "wkv_u": np.concatenate([wkv_units(np.asarray(L0_xattn_wk)), wkv_units(np.asarray(L0_xattn_wv))], 1),
        "wq_u": np.asarray(L0_xattn_wq).reshape(CH, P, HKV, UW).transpose(2, 0, 1, 3),
        "wo_u": np.asarray(L0_xattn_wo).reshape(HKV, G, P, 2, UW).transpose(0, 1, 3, 2, 4).reshape(HKV, W_U, P, UW),
        "tab_f": c["tab_f"], "tab_i": c["tab_i"], "cos_k": c["cos_k"], "sin_k": c["sin_k"],
        "cos_q": c["cos_q"], "sin_q": c["sin_q"], "ident_d": c["ident"],
        "aw": np.concatenate([np.asarray(L0_ffn_Wr).T, np.asarray(L0_ffn_A).reshape(E * R, D).T], 1)
        .reshape(CH, P, E + E * R).transpose(1, 0, 2).reshape(P, CH * (E + E * R)),
        "bt": np.asarray(L0_ffn_B).transpose(0, 2, 1).reshape(E * R, D),
        "iota_d": c["iota"],
    }
    arrays = {k: np.ascontiguousarray(v) for k, v in arrays.items()}
    nc = bacc.Bacc("TRN2", target_bir_lowering=False, num_devices=1)
    args = {k: nc.dram_tensor(k + "_dram", list(v.shape), mybir.dt.from_np(v.dtype), kind="ExternalInput").ap()
            for k, v in arrays.items()}
    out = nc.dram_tensor("out_dram", [T, D], F32, kind="ExternalOutput").ap()
    perceiver_kernel(nc, out=out, **args)
    r = run_bass_kernel_spmd(nc, [{k + "_dram": v for k, v in arrays.items()}], core_ids=[0])
    return r.results[0]["out_dram"].reshape(B, SQ, D)
```

```python
from contextlib import ExitStack

import numpy as np

import concourse.bass as bass
from concourse import mybir

ALU = mybir.AluOpType
ACT = mybir.ActivationFunctionType
F32 = mybir.dt.float32
F32R = mybir.dt.float32r
I32 = mybir.dt.int32
U32 = mybir.dt.uint32

P = 128
B, SQ, D = 2, 64, 1024
SK = 1024
HQ, HKV, DK = 32, 8, 128
G = HQ // HKV
T = B * SQ
CH = D // P
UW = 512
KB = SK // UW
STEPS = B * HKV
RING = 6
HALF = D // 2
LAGS = HALF // 2 + 2
SLOT = max(UW, 2 * LAGS)
F_COLS = CH * UW
E, R = 4, 16
LORA_SCALE = 16.0 / np.sqrt(16.0)
EPS = 1e-5
TOPK = 6
LOWEST = -3.0e38

WK_U, WV_U, W_U, CTX_U = 2, 2, 8, KB * CH
FIRST_W = WK_U + WV_U + CTX_U
FIRST_WK1 = FIRST_W + W_U
PRO_U = FIRST_WK1 + WK_U
X_AFTER = 16
STEP_U = W_U + WV_U + WK_U
CTX1 = PRO_U + STEP_U * (HKV - 1)
STEP7_U = CTX1 + CH
BASE1 = STEP7_U + STEP_U
STEP15_U = BASE1 + STEP_U * (HKV - 1) - WK_U
TAB_U = STEP15_U + W_U
INV_U = TAB_U + CH // 2
assert STEP_U % RING == 0


def first_unit(kind, j):
    return {"wk": (0, 6), "wv": (2, 7), "ctx": (1, 3, 4, 5, *range(8, 4 + CTX_U))}[kind][j]


PROLOGUE = sorted((first_unit(kind, j), kind, j) for kind, n in (("wk", WK_U), ("wv", WV_U), ("ctx", CTX_U))
                  for j in range(n))


class Step:

    def __init__(self, s, at):
        self.s, self.slope = s, STEP_U
        if at < HKV - 1:
            self.first = PRO_U
        elif at == HKV - 1:
            self.first, self.slope = STEP7_U, 0
        elif at <= STEPS - 2:
            self.first = BASE1 - STEP_U * HKV
        else:
            self.first, self.slope = STEP15_U, 0

    def w(self, j):
        return Unit(self.first + j, self.slope, self.s)

    def wv(self, j):
        return self.w(W_U + j)

    def wk(self, j):
        return self.w(W_U + WV_U + j)


class Unit:

    def __init__(self, static, slope=0, s=0):
        self.static, self.slope, self.s = static, slope, s
        self.slot = static % RING

    def count(self, plus):
        return self.static + plus + (self.slope * self.s if self.slope else 0)

    def arrivals(self):
        return 16 * (self.static // RING + 1) + (16 * (self.slope // RING) * self.s if self.slope else 0)


def perceiver_kernel(nc, x, ctx_u, mask, wkv_u, wq_u, wo_u, tab_e, tab_o, tab_i, cos_k, sin_k, cos_q, sin_q,
                     ident_d, aw, bt, iota_d, out):
    with ExitStack() as stack:
        def sb(name, cols, dt=F32, rows=P):
            return stack.enter_context(nc.sbuf_tensor(name, [rows, cols], dt))

        def pb(name):
            return stack.enter_context(nc.psum_tensor(name, [P, 2 * UW], F32))

        def sem(name):
            return stack.enter_context(nc.semaphore(name))

        ctx_hi, ctx_lo = sb("ctx_hi", CTX_U * UW, F32R), sb("ctx_lo", CTX_U * UW, F32R)
        wk_hi, wk_lo = sb("wk_hi", CH * P, F32R), sb("wk_lo", CH * P, F32R)
        wv_hi, wv_lo = sb("wv_hi", CH * P, F32R), sb("wv_lo", CH * P, F32R)
        w_hi, w_lo = sb("w_hi", W_U * UW, F32R), sb("w_lo", W_U * UW, F32R)
        raw = sb("raw", RING * SLOT)
        k_hi, k_lo = sb("k_hi", SK, F32R), sb("k_lo", SK, F32R)
        v_hi, v_lo = sb("v_hi", SK, F32R), sb("v_lo", SK, F32R)
        soft = sb("soft", 2 * SK)
        pt_hi, pt_lo = sb("pt_hi", 2 * UW, F32R), sb("pt_lo", 2 * UW, F32R)
        cosk, sink = sb("cosk", SK), sb("sink", SK)
        cosq, sinq = sb("cosq", DK), sb("sinq", DK)
        maskt = sb("maskt", SK)
        q1 = sb("q1", HKV * G * SQ)
        o0 = sb("o0", HKV * G * SQ)
        q_hi, q_lo = sb("q_hi", G * SQ, F32R), sb("q_lo", G * SQ, F32R)
        o_hi, o_lo = sb("o_hi", G * T, F32R), sb("o_lo", G * T, F32R)
        xt_hi, xt_lo = sb("xt_hi", CH * T, F32R), sb("xt_lo", CH * T, F32R)
        krot, kswap = sb("krot", KB * UW), sb("kswap", UW)
        ident = sb("ident", P)
        ones = sb("ones", 2)
        st = sb("st", 144)
        top8, top_e = sb("top8", 8), sb("top_e", 8)
        flag_i = sb("flag_i", 2, I32)
        idx8, idx_e = sb("idx8", 8, U32), sb("idx_e", 8, U32)

        mx, nm, rs, ri = st[:, 0:4], st[:, 4:6], st[:, 6:8], st[:, 132:134]
        gap, near, top_neg, spare = st[:, 134:135], st[:, 135:136], st[:, 136:137], st[:, 137:138]
        grown = st[:, 138:139]
        lg, ex, sel, gs = st[:, 28:36], st[:, 36:40], st[:, 40:48], st[:, 48:52]
        idxf, iota4 = st[:, 52:60], st[:, 60:64]
        gate = st[:, 108:112]
        ln_cols = (st[:, 8:28], st[:, 112:132])
        neg0, e8 = st[:, 94:95], st[:, 96:104]
        gsum, grec = st[:, 64:65], st[:, 65:66]

        pk = pb("pk")
        pa = pb("pa")
        ps = pb("ps")
        py = pb("py")

        raw_in = [sem(f"raw_in{i}") for i in range(RING)]
        x_in, tab_in, mask_in, late_in, out_done = (
            sem(n) for n in ("x_in", "tab_in", "mask_in", "late_in", "out_done"))
        qtab_in, even_in = sem("qtab_in"), sem("even_in")
        unit_hi, unit_lo = sem("unit_hi"), sem("unit_lo")
        ones_set = sem("ones_set")
        ln_bn, ln_ag, ln_var, ln_rstd, ln_out = (sem(n) for n in ("ln_bn", "ln_ag", "ln_var", "ln_rstd", "ln_out"))
        ln_sd = sem("ln_sd")
        xt_ps, xt_h, xt_l, seeded = sem("xt_ps"), sem("xt_h"), sem("xt_l"), sem("seeded")
        kproj, k_mul, k_rot, k_h, k_l = sem("kproj"), sem("k_mul"), sem("k_rot"), sem("k_h"), sem("k_l")
        vproj, vt_raw, vtr, v_h, v_l = sem("vproj"), sem("vt_raw"), sem("vtr"), sem("v_h"), sem("v_l")
        qproj, q_mul, q_rot, qtr, q_h, q_l = (sem(n) for n in ("qproj", "q_mul", "q_rot", "qtr", "q_h", "q_l"))
        scored, masked, nmax, expd, recip, prob = (
            sem(n) for n in ("scored", "masked", "nmax", "expd", "recip", "prob"))
        ptr, pt_h, pt_l, pv = sem("ptr"), sem("pt_h"), sem("pt_l"), sem("pv")
        o_raw, o_h, o_l, w_used = sem("o_raw"), sem("o_h"), sem("o_l"), sem("w_used")
        fold, ab_ps, ab_h, ab_l, dft = sem("fold"), sem("ab_ps"), sem("ab_h"), sem("ab_l"), sem("dft")
        sq, sq_ps, sq_h, sq_l, idft = sem("sq"), sem("sq_ps"), sem("sq_h"), sem("sq_l"), sem("idft")
        even_out, lagged, topped, gapped, near_ps, flagged = (
            sem(n) for n in ("even_out", "lagged", "topped", "gapped", "near_ps", "flagged"))
        x2_done, h_ps, h_t, lora, lg_in, lg_top, g_exp, g_step, mid_ps, mid_t, delta, y_out = (
            sem(n) for n in ("x2_done", "h_ps", "h_t", "lora", "lg_in", "lg_top", "g_exp", "g_step", "mid_ps",
                             "mid_t", "delta", "y_out"))
        h_t1 = sem("h_t1")
        weighed, sqrt_set, exp_set, x1_copy = sem("weighed"), sem("sqrt_set"), sem("exp_set"), sem("x1_copy")
        x2_stat = sem("x2_stat")
        gen, top_out = sem("gen"), sem("top_out")

        def raw_ap(u, cols=UW):
            return raw[:, u.slot * SLOT:u.slot * SLOT + cols]

        def ln_part(n):
            c = ln_cols[0 if n <= 2 else 1]
            return dict(bn=c[:, 0:12], ag=c[:, 12:14], rstd=c[:, 14:15], ve=c[:, 15:16], sd=c[:, 16:17],
                        rec=c[:, 17:18], nwt=c[:, 18:19])

        def blk(t, i, w=UW):
            return t[:, i * w:(i + 1) * w]

        block = stack.enter_context(nc.Block())

        @block.sync
        def _(sp):
            def load_unit(u, src, wait=True, cols=UW):
                if wait:
                    sp.wait_ge(unit_lo, u.count(1 - RING))
                sp.dma_start(raw_ap(u, cols), src).then_inc(raw_in[u.slot], 16)

            def load_pro(n, src):
                load_unit(Unit(n), src, wait=n >= RING)

            def load_wv(step, head):
                for i in range(WV_U):
                    load_unit(step.wv(i), wkv_u[head, WK_U + i])

            def load_wk(step, head):
                for i in range(WK_U):
                    load_unit(step.wk(i), wkv_u[head, i])

            def load_w(step, table, head):
                for j in range(W_U):
                    load_unit(step.w(j), table[head, j])

            def load_mask(b):
                for h in range(2):
                    sp.dma_start(maskt[h * SQ:(h + 1) * SQ, :], mask[b]).then_inc(mask_in, 16)

            for n, kind, j in PROLOGUE:
                load_pro(n, ctx_u[0, j] if kind == "ctx" else wkv_u[0, j + (WK_U if kind == "wv" else 0)])
                if n == X_AFTER:
                    sp.dma_start(soft[:, 0:D], x).then_inc(x_in, 16)
                    sp.dma_start(ident[:, :], ident_d).then_inc(x_in, 16)
            sp.dma_start(cosk[:, :], cos_k).then_inc(tab_in, 16)
            sp.dma_start(sink[:, :], sin_k).then_inc(tab_in, 16)
            for i in range(W_U):
                load_pro(FIRST_W + i, wq_u[0, i])
            sp.dma_start(cosq[:, :], cos_q).then_inc(qtab_in, 16)
            sp.dma_start(sinq[:, :], sin_q).then_inc(qtab_in, 16)
            load_mask(0)
            for i in range(WK_U):
                load_pro(FIRST_WK1 + i, wkv_u[1, i])

            with sp.Fori(0, HKV - 2) as s:
                step = Step(s, 0)
                load_w(step, wq_u, s + 1)
                load_wv(step, s + 1)
                load_wk(step, s + 2)
            step = Step(HKV - 2, HKV - 2)
            load_w(step, wq_u, HKV - 1)
            load_wv(step, HKV - 1)
            load_wk(step, 0)
            for i in range(CH):
                load_unit(Unit(CTX1 + i), ctx_u[1, i])
            step = Step(HKV - 1, HKV - 1)
            for i in range(CH):
                load_unit(step.w(i), ctx_u[1, CH + i])
            load_wv(step, 0)
            load_wk(step, 1)
            sp.wait_ge(masked, 4 * HKV)
            load_mask(1)
            with sp.Fori(HKV, STEPS - 2) as s:
                step = Step(s, HKV)
                load_w(step, wo_u, s - HKV)
                load_wv(step, s - HKV + 1)
                load_wk(step, s - HKV + 2)
            step = Step(STEPS - 2, STEPS - 2)
            load_w(step, wo_u, HKV - 2)
            load_wv(step, HKV - 1)
            load_w(Step(STEPS - 1, STEPS - 1), wo_u, HKV - 1)
            for i in range(CH // 2):
                load_unit(Unit(TAB_U + i), tab_o[i])
            for i in range(CH // 2):
                load_unit(Unit(INV_U + i), tab_i[i], cols=2 * LAGS)
            sp.wait_ge(k_rot, KB * STEPS)
            sp.dma_start(cosk[0:E * R, :], bt).then_inc(late_in, 16)
            sp.dma_start(sink[:, 0:CH * (E + E * R)], aw).then_inc(late_in, 16)
            sp.dma_start(iota4, iota_d).then_inc(late_in, 16)

            def store(n):
                for i in range(2):
                    sp.wait_ge(y_out, 2 * n + i - 1)
                    sp.dma_start(out[:, i * UW:(i + 1) * UW], blk(soft, i)).then_inc(out_done, 16)

            store(1)
            sp.wait_ge(flagged, 1)
            rows_near = sp.value_load(flag_i[0:1, 0:1], min_val=0, max_val=P)
            sp.wait_ge(out_done, 32)
            with sp.If(rows_near > 0):
                store(2)
                sp.wait_ge(out_done, 64)

        @block.gpsimd
        def _(pool):
            pool.wait_ge(vproj, KB * STEPS - 1)
            for part, dst in enumerate((ctx_hi, ctx_lo)):
                pool.dma_start(dst[:, 0:F_COLS // 2], tab_e[part]).then_inc(even_in, 16)

        @block.tensor
        def _(pe):
            def product(acc, st_hi, st_lo, mv_hi, mv_lo, first, last):
                nc.tensor.matmul(acc, st_lo, mv_hi, start=first, stop=False)
                nc.tensor.matmul(acc, st_hi, mv_lo, start=False, stop=False)
                return nc.tensor.matmul(acc, st_hi, mv_hi, start=False, stop=last)

            def project(acc, hi, lo, b, chunks=range(CH), ctx_at=None):
                for c in chunks:
                    if ctx_at is not None:
                        pe.wait_ge(unit_lo, ctx_at(c) + 1)
                    mm = product(acc, blk(hi, c, P), blk(lo, c, P), blk(ctx_hi, b * CH + c),
                                 blk(ctx_lo, b * CH + c), c == 0, c == CH - 1)
                return mm

            def k_project(m, b, wk_ready=None, chunks=range(CH), ctx_at=None, again=True):
                if wk_ready is not None:
                    pe.wait_ge(unit_lo, wk_ready)
                if again and 0 in chunks:
                    pe.wait_ge(k_rot, KB * m + b - 1)
                mm = project(blk(pk, b), wk_hi, wk_lo, b, chunks, ctx_at)
                if CH - 1 in chunks:
                    mm.then_inc(kproj, 1)

            def v_project(m, b, wv_ready=None, chunks=range(CH), again=True):
                if wv_ready is not None:
                    pe.wait_ge(unit_lo, wv_ready)
                if again:
                    pe.wait_ge(pt_l, 4 * m + b - 1)
                mm = project(blk(pa, b), wv_hi, wv_lo, b, chunks)
                if CH - 1 in chunks:
                    mm.then_inc(vproj, 1)

            def v_transposes(m, b):
                pe.wait_ge(vt_raw, KB * m + b + 1)
                for c in range(4):
                    mm = nc.tensor.transpose(pa[:, b * UW + c * P:b * UW + (c + 1) * P],
                                             soft[:, b * UW + c * P:b * UW + (c + 1) * P], ident[:, :])
                mm.then_inc(vtr, 1)

            def q_project(m, unit_at, again=True):
                if again:
                    pe.wait_ge(masked, 4 * m)
                for c in range(CH):
                    pe.wait_ge(unit_lo, unit_at(c).count(1))
                    mm = product(blk(ps, 1), blk(xt_hi, c, P), blk(xt_lo, c, P), blk(w_hi, c), blk(w_lo, c),
                                 c == 0, c == CH - 1)
                mm.then_inc(qproj, 1)

            def q_transposes(m, again=True):
                pe.wait_ge(q_rot, m + 1)
                if again:
                    pe.wait_ge(o_raw, m)
                for h in range(G):
                    mm = nc.tensor.transpose(blk(ps, h, P), soft[:, SK + h * P:SK + (h + 1) * P], ident[:, :])
                mm.then_inc(qtr, 1)

            def scores(s, o_left=None, pause=None):
                pe.wait_ge(q_l, s + 1)
                if o_left is not None:
                    pe.wait_ge(*o_left)
                for i in range(4):
                    t, b = divmod(i, 2)
                    if t == 0:
                        pe.wait_ge(k_l, KB * s + b + 1)
                    else:
                        pe.wait_ge(masked, 4 * s + i - 1)
                    product(blk(ps, b), blk(q_hi, t, P), blk(q_lo, t, P), blk(k_hi, b), blk(k_lo, b),
                            True, True).then_inc(scored, 1)
                    if i == 0:
                        v_transposes(s, 1)
                    elif i == 1 and pause is not None:
                        pause()

            def turn(s, i):
                if i == 0:
                    pe.wait_ge(prob, 2 * s + 2)
                if i < 2:
                    pe.wait_ge(v_l, KB * s + i + 1)
                else:
                    pe.wait_ge(pt_l, 4 * s + i - 1)
                for c in range(2):
                    for t in range(2):
                        mm = nc.tensor.transpose(
                            pa[:, (i % 2) * UW + c * 256 + t * P:(i % 2) * UW + c * 256 + (t + 1) * P],
                            soft[:, t * SK + (2 * i + c) * P:t * SK + (2 * i + c + 1) * P], ident[:, :])
                mm.then_inc(ptr, 1)

            def weigh(s, i):
                pe.wait_ge(pt_l, 4 * s + i + 1)
                for c in range(2):
                    k, m = 2 * i + c, (i % 2) * UW + c * 256
                    mm = product(ps[:, 0:G * SQ], blk(v_hi, k, P), blk(v_lo, k, P), pt_hi[:, m:m + 256],
                                 pt_lo[:, m:m + 256], k == 0, k == CH - 1)
                mm.then_inc(pv, 1)

            def attend_and_k(s, wk_ready, ctx_at=(None, None)):
                scores(s, pause=lambda: k_project(s + 1, 0, wk_ready, chunks=(0,), ctx_at=ctx_at[0]))
                k_project(s + 1, 0, chunks=range(1, CH), ctx_at=ctx_at[0])
                turn(s, 0)
                turn(s, 1)
                k_project(s + 1, 1, chunks=range(0, CH // 2), ctx_at=ctx_at[1])
                weigh(s, 0)
                turn(s, 2)
                weigh(s, 1)
                turn(s, 3)
                k_project(s + 1, 1, chunks=range(CH // 2, CH), ctx_at=ctx_at[1])
                weigh(s, 2)
                weigh(s, 3)

            def out_project(s, unit_at, final, js=range(W_U)):
                pe.wait_ge(o_l, s - HKV + 1)
                for j in js:
                    h, n = divmod(j, 2)
                    pe.wait_ge(unit_lo, unit_at(j).count(1))
                    mm = product(blk(py, n), blk(o_hi, h, T), blk(o_lo, h, T), blk(w_hi, j), blk(w_lo, j),
                                 False, final and h == G - 1)
                if W_U - 1 in js:
                    mm.then_inc(w_used, 1)

            for c in range(CH):
                k_project(0, 0, chunks=(c,), ctx_at=lambda c: first_unit("ctx", c), again=False)
                v_project(0, 0, first_unit("wv", c // 4) + 1, chunks=(c,), again=False)
            k_project(0, 1, ctx_at=lambda c: first_unit("ctx", CH + c), again=False)
            pe.wait_ge(x_in, 32)
            for n in range(2):
                mm = nc.tensor.matmul(blk(py, n), ident[:, :], blk(soft, n), start=True, stop=False)
            mm.then_inc(seeded, 1)
            pe.wait_ge(ln_out, 1)
            for n in range(2):
                for c in range(4):
                    mm = nc.tensor.transpose(ps[:, n * UW + c * P:n * UW + (c + 1) * P],
                                             soft[:, D + n * UW + c * P:D + n * UW + (c + 1) * P], ident[:, :])
                mm.then_inc(xt_ps, 1)
            v_project(0, 1, chunks=range(0, 3), again=False)
            pe.wait_ge(xt_l, 2)
            q_project(0, lambda j: Unit(FIRST_W + j), again=False)
            v_project(0, 1, chunks=range(3, 7), again=False)
            q_transposes(0, again=False)
            v_project(0, 1, chunks=range(7, CH), again=False)
            v_transposes(0, 0)

            def step_0(s, at):
                step = Step(s, at)
                attend_and_k(s, step.w(0).count(0))
                q_project(s + 1, step.w)
                v_project(s + 1, 0, step.wv(1).count(1))
                q_transposes(s + 1)
                v_project(s + 1, 1)
                v_transposes(s + 1, 0)

            with pe.Fori(0, HKV - 2) as s:
                step_0(s, 0)
            step_0(HKV - 2, HKV - 2)
            s = HKV - 1
            step = Step(s, s)
            attend_and_k(s, None, (lambda c: CTX1 + c, lambda c: STEP7_U + c))
            v_project(s + 1, 0, step.wv(1).count(1))
            v_project(s + 1, 1)
            v_transposes(s + 1, 0)

            def step_1(s, at, project_o=True):
                step = Step(s, at)
                attend_and_k(s, step.w(0).count(0))
                v_project(s + 1, 0, step.wv(1).count(1))
                if project_o:
                    out_project(s, step.w, final=False)
                v_project(s + 1, 1)
                v_transposes(s + 1, 0)

            with pe.Fori(HKV, STEPS - 2) as s:
                step_1(s, HKV)
            s = STEPS - 2
            step_1(s, s, project_o=False)
            scores(s + 1, (o_l, HKV - 1))
            out_project(s, Step(s, s).w, final=False, js=range(0, 6))
            turn(s + 1, 0)
            turn(s + 1, 1)
            out_project(s, Step(s, s).w, final=False, js=range(6, W_U))
            s = STEPS - 1
            for i in range(4):
                weigh(s, i)
                if i < 2:
                    turn(s, i + 2)
            out_project(s, Step(s, s).w, final=True)

            def transposes(dst, src, done):
                for c in range(4):
                    mm = nc.tensor.transpose(blk(dst, c, P), blk(src, c, P), ident[:, :])
                mm.then_inc(done, 1)

            def transform(acc, part, hi, lo, at, w, done, chunks=range(4)):
                for c in chunks:
                    j = 4 * part + c
                    k = at + j * w
                    mm = product(acc[:, 0:w], blk(hi, j, P), blk(lo, j, P), ctx_hi[:, k:k + w], ctx_lo[:, k:k + w],
                                 c == 0, c == 3)
                if 3 in chunks:
                    mm.then_inc(done, 1)

            def experts(n):
                W = E + E * R
                for c in range(CH):
                    if c % 4 == 0:
                        pe.wait_ge((h_t, h_t1)[c // 4], n)
                    mm = nc.tensor.matmul(pa[:, UW:UW + W], blk(maskt, c, P), sink[:, c * W:(c + 1) * W],
                                          start=c == 0, stop=c == CH - 1)
                mm.then_inc(lora, 1)

            def experts_out(n):
                pe.wait_ge(g_step, 6 * n)
                nc.tensor.transpose(pa[0:E * R, 0:P], kswap[:, 0:E * R], ident[:, :]).then_inc(mid_ps, 1)
                pe.wait_ge(mid_t, n)
                for h in range(2):
                    nc.tensor.matmul(blk(pk, h), kswap[0:E * R, 128:256], cosk[0:E * R, h * UW:(h + 1) * UW],
                                     start=True, stop=True).then_inc(delta, 1)

            pe.wait_ge(fold, 1)
            transposes(blk(pk, 1), blk(q1, 3), ab_ps)
            pe.wait_ge(ab_l, 1)
            pe.wait_ge(unit_lo, INV_U)
            transform(blk(pa, 1), 1, xt_hi, xt_lo, 0, UW, dft, range(0, 3))
            pe.wait_ge(fold, 2)
            transposes(blk(pk, 0), blk(q1, 2), ab_ps)
            transform(blk(pa, 1), 1, xt_hi, xt_lo, 0, UW, dft, range(3, 4))
            pe.wait_ge(ln_out, 3)
            for h in range(2):
                transposes(blk(ps, h), blk(soft, 2 + h), h_ps)
            pe.wait_ge(sq, 1)
            transposes(blk(pk, 1), blk(o0, 1), sq_ps)
            pe.wait_ge(ab_l, 2)
            pe.wait_ge(even_in, 32)
            transform(blk(pa, 0), 0, xt_hi, xt_lo, 0, UW, dft)
            pe.wait_ge(late_in, 48)
            experts(1)
            pe.wait_ge(sq, 2)
            transposes(blk(pk, 0), blk(o0, 0), sq_ps)
            pe.wait_ge(unit_lo, INV_U + CH // 2)
            for n, part in enumerate((1, 0)):
                pe.wait_ge(sq_l, n + 1)
                transform(blk(ps, part), part, k_hi, k_lo, F_COLS, LAGS, idft)
            experts_out(1)
            pe.wait_ge(gapped, 3)
            nc.tensor.matmul(ps[0:1, UW - 1:UW], near, ones[:, 0:1], start=True, stop=True).then_inc(near_ps, 1)
            pe.wait_ge(flagged, 1)
            rows_near = pe.value_load(flag_i[0:1, 0:1], min_val=0, max_val=P)
            with pe.If(rows_near > 0):
                pe.wait_ge(ln_out, 4)
                for h in range(2):
                    transposes(blk(ps, h), blk(soft, 2 + h), h_ps)
                experts(2)
                experts_out(2)

        @block.scalar
        def _(act):
            def unit(u, dst, free=None, cols=UW):
                if free is not None:
                    act.wait_ge(*free)
                act.wait_ge(raw_in[u.slot], u.arrivals())
                nc.scalar.copy(dst, raw_ap(u, cols)).then_inc(unit_hi, 1)

            def root(n):
                act.wait_ge(ln_var, n)
                c = ln_part(n)
                nc.scalar.activation(c["sd"], c["ve"], ACT.Sqrt).then_inc(ln_sd, 1)

            def k_his(m, again=True):
                for b in range(KB):
                    act.wait_ge(k_rot, KB * m + b + 1)
                    if again:
                        act.wait_ge(scored, 4 * m)
                    nc.scalar.copy(blk(k_hi, b), blk(krot, b)).then_inc(k_h, 1)

            def vt_copy(m, b):
                act.wait_ge(vproj, KB * m + b + 1)
                nc.scalar.copy(blk(soft, b), blk(pa, b)).then_inc(vt_raw, 1)

            def v_his(m, again=True):
                for b in range(KB):
                    act.wait_ge(vtr, KB * m + b + 1)
                    if again:
                        act.wait_ge(pv, 4 * m)
                    nc.scalar.copy(blk(v_hi, b), blk(pa, b)).then_inc(v_h, 1)

            def q_his_0(m, again=True):
                act.wait_ge(qtr, m + 1)
                if again:
                    act.wait_ge(scored, 4 * m)
                src = blk(ps, 0).rearrange("p (h b t) -> p b h t", h=G, b=B)
                nc.scalar.copy(q_hi.rearrange("p (h t) -> p h t", h=G), src[:, 0]).then_inc(q_h, 1)
                nc.scalar.copy(q1[:, bass.ds(m * (G * SQ), G * SQ)].rearrange("p (h t) -> p h t", h=G),
                               src[:, 1]).then_inc(q_h, 1)

            def q_his_1(m):
                act.wait_ge(scored, 4 * m)
                nc.scalar.copy(q_hi[:, :], q1[:, bass.ds((m - HKV) * (G * SQ), G * SQ)]).then_inc(q_h, 2)

            def softmax_exp(s):
                for t in range(2):
                    act.wait_ge(nmax, 2 * s + t + 1)
                    nc.scalar.activation(blk(soft, t, SK), blk(soft, t, SK), ACT.Exp, bias=nm[:, t:t + 1],
                                         scale=1.0, accum_out=rs[:, t:t + 1]).then_inc(expd, 1)

            def pt_his(s, turns, first=False):
                for i in turns:
                    act.wait_ge(ptr, 4 * s + i + 1)
                    if i >= 2 or not first:
                        act.wait_ge(pv, 4 * s + i - 1)
                    nc.scalar.copy(blk(pt_hi, i % 2), blk(pa, i % 2)).then_inc(pt_h, 1)

            def keep_o(s):
                act.wait_ge(pv, 4 * s + 4)
                nc.scalar.copy(o0[:, bass.ds(s * (G * SQ), G * SQ)], ps[:, 0:G * SQ]).then_inc(o_raw, 1)

            oh = o_hi.rearrange("p (h b t) -> p b h t", h=G, b=B)

            def o_hi_0(s, first=False):
                if not first:
                    act.wait_ge(w_used, s - HKV)
                nc.scalar.copy(oh[:, 0], o0[:, bass.ds((s - HKV) * (G * SQ), G * SQ)]
                               .rearrange("p (h t) -> p h t", h=G)).then_inc(o_h, 1)

            def o_hi_1(s):
                act.wait_ge(pv, 4 * s + 4)
                nc.scalar.copy(oh[:, 1], ps[:, 0:G * SQ].rearrange("p (h t) -> p h t", h=G)).then_inc(o_h, 1)

            def w_units(units, dst, free):
                for j, (u, at) in enumerate(units):
                    unit(u, blk(dst, at), free if j == 0 else None)

            for n, kind, j in PROLOGUE:
                unit(Unit(n), blk({"wk": wk_hi, "wv": wv_hi, "ctx": ctx_hi}[kind], j))
            root(1)
            for j in range(4):
                unit(Unit(FIRST_W + j), blk(w_hi, j))
            for n in range(2):
                act.wait_ge(xt_ps, n + 1)
                nc.scalar.copy(blk(xt_hi, n), blk(ps, n)).then_inc(xt_h, 1)
            for j in range(4, W_U):
                unit(Unit(FIRST_W + j), blk(w_hi, j))
            k_his(0, again=False)
            act.wait_ge(seeded, 1)
            act.wait_ge(ln_out, 1)
            vt_copy(0, 0)
            q_his_0(0, again=False)
            vt_copy(0, 1)
            for j in range(WK_U):
                unit(Unit(FIRST_WK1 + j), blk(wk_hi, j), (kproj, KB))

            def step_act(s, at, batch, w_free, first=False):
                step = Step(s, at)
                w_dst, w_at = (ctx_hi, CH) if at == HKV - 1 else (w_hi, 0)
                v_his(s, again=at > 0)
                softmax_exp(s)
                if at == STEPS - 1:
                    act.wait_ge(ones_set, 1)
                    nc.scalar.activation(spare, ones[:, 0:1], ACT.Sqrt).then_inc(sqrt_set, 1)
                    pt_his(s, (0, 1))
                    o_hi_0(s)
                    w_units([(step.w(0), 0)], w_hi, w_free)
                    pt_his(s, (2,))
                    w_units([(step.w(1), 1)], w_hi, None)
                    pt_his(s, (3,))
                    w_units([(step.w(j), j) for j in range(2, 4)], w_hi, None)
                    o_hi_1(s)
                    w_units([(step.w(j), j) for j in range(4, W_U)], w_hi, None)
                    return
                if batch == 1:
                    o_hi_0(s, first)
                w_units([(step.w(j), w_at + j) for j in range(4)], w_dst, w_free)
                pt_his(s, (0, 1), first=at == 0)
                w_units([(step.w(j), w_at + j) for j in range(4, W_U)], w_dst, None)
                w_units([(step.wv(j), j) for j in range(WV_U)], wv_hi, (vproj, KB * (s + 1)))
                pt_his(s, (2, 3))
                if batch == 0:
                    keep_o(s)
                else:
                    o_hi_1(s)
                k_his(s + 1)
                if at < STEPS - 2:
                    w_units([(step.wk(j), j) for j in range(WK_U)], wk_hi, (kproj, KB * (s + 2)))
                vt_copy(s + 1, 0)
                if at < HKV - 1:
                    q_his_0(s + 1)
                else:
                    if at == HKV - 1:
                        act.wait_ge(q_h, 2 * HKV)
                    q_his_1(s + 1)
                if at == HKV - 2:
                    w_units([(Unit(CTX1 + j), j) for j in range(CH)], ctx_hi, (vproj, KB * (s + 1) + 1))
                vt_copy(s + 1, 1)

            step_act(0, 0, 0, (qproj, 1))
            with act.Fori(1, HKV - 2) as s:
                step_act(s, 1, 0, (qproj, s + 1))
            step_act(HKV - 2, HKV - 2, 0, (qproj, HKV - 1))
            step_act(HKV - 1, HKV - 1, 0, (vproj, KB * HKV))
            step_act(HKV, HKV, 1, (qproj, HKV), True)
            with act.Fori(HKV + 1, STEPS - 2) as s:
                step_act(s, HKV + 1, 1, (w_used, s - HKV))
            step_act(STEPS - 2, STEPS - 2, 1, (w_used, HKV - 2))
            step_act(STEPS - 1, STEPS - 1, 1, (w_used, HKV - 1))

            for j in range(CH // 2):
                unit(Unit(TAB_U + j), blk(ctx_hi, CH // 2 + j))

            act.wait_ge(w_used, HKV)
            nc.scalar.copy(blk(q1, 3), blk(py, 1)).then_inc(x1_copy, 1)
            act.wait_ge(ab_ps, 1)
            nc.scalar.copy(blk(xt_hi, 1), blk(pk, 1)).then_inc(ab_h, 1)
            root(2)
            root(3)
            for j in range(CH // 2):
                unit(Unit(INV_U + j), blk(ctx_hi[:, F_COLS:], j, 2 * LAGS), cols=2 * LAGS)
            act.wait_ge(ab_ps, 2)
            nc.scalar.copy(blk(xt_hi, 0), blk(pk, 0)).then_inc(ab_h, 1)
            act.wait_ge(dft, 1)
            act.wait_ge(ln_rstd, 8)
            nc.scalar.activation(blk(o0, 1), blk(pa, 1), ACT.Square, scale=ln_part(2)["rstd"]).then_inc(sq, 1)
            act.wait_ge(h_ps, 1)
            nc.scalar.copy(blk(maskt, 0), blk(ps, 0)).then_inc(h_t, 1)
            act.wait_ge(sq_ps, 1)
            nc.scalar.copy(blk(k_hi, 1), blk(pk, 1)).then_inc(sq_h, 1)
            act.wait_ge(sqrt_set, 1)
            nc.scalar.activation(spare, ones[:, 0:1], ACT.Exp).then_inc(exp_set, 1)
            act.wait_ge(dft, 2)
            nc.scalar.activation(blk(o0, 0), blk(pa, 0), ACT.Square).then_inc(sq, 1)
            act.wait_ge(sq_ps, 2)
            nc.scalar.copy(blk(k_hi, 0), blk(pk, 0)).then_inc(sq_h, 1)
            act.wait_ge(lg_top, 1)
            nc.scalar.activation(ex, lg[:, 0:E], ACT.Exp, bias=top_neg, scale=1.0).then_inc(g_exp, 1)
            act.wait_ge(idft, 2)
            nc.scalar.copy(krot[:, 0:LAGS], ps[:, 0:LAGS]).then_inc(even_out, 1)
            act.wait_ge(flagged, 1)
            rows_near = act.value_load(flag_i[0:1, 0:1], min_val=0, max_val=P)
            with act.If(rows_near > 0):
                nc.scalar.activation(e8, top8[:, :], ACT.Exp, bias=neg0, scale=1.0).then_inc(weighed, 1)
                root(4)
                act.wait_ge(h_ps, 3)
                nc.scalar.copy(blk(maskt, 0), blk(ps, 0)).then_inc(h_t, 1)
                act.wait_ge(lg_top, 2)
                nc.scalar.activation(ex, lg[:, 0:E], ACT.Exp, bias=top_neg, scale=1.0).then_inc(g_exp, 1)

        @block.vector
        def _(dve):
            def unit(u, hi, lo, at, first=0, cols=UW):
                dve.wait_ge(unit_hi, u.count(1))
                nc.vector.tensor_tensor(blk(lo[:, first:], at, cols), raw_ap(u, cols), blk(hi[:, first:], at, cols),
                                        ALU.subtract).then_inc(unit_lo, 1)

            def lo(dst_lo, src, hi, done, ready=None):
                if ready is not None:
                    dve.wait_ge(*ready)
                nc.vector.tensor_tensor(dst_lo, src, hi, ALU.subtract).then_inc(done, 1)

            def inverse_root(n):
                c = ln_part(n)
                dve.wait_ge(ln_sd, n)
                nc.vector.reciprocal(c["rec"], c["sd"]).then_inc(ln_rstd, 1)
                dve.wait_ge(ln_rstd, 4 * n - 3)
                nc.vector.scalar_tensor_tensor(out=c["nwt"], in0=c["rec"], scalar=c["rec"], in1=c["ve"],
                                               op0=ALU.mult, op1=ALU.mult).then_inc(ln_rstd, 1)
                dve.wait_ge(ln_rstd, 4 * n - 2)
                nc.vector.tensor_scalar(c["nwt"], c["nwt"], -0.5, 1.5, ALU.mult, ALU.add).then_inc(ln_rstd, 1)
                dve.wait_ge(ln_rstd, 4 * n - 1)
                nc.vector.tensor_tensor(c["rstd"], c["rec"], c["nwt"], ALU.mult).then_inc(ln_rstd, 1)
                dve.wait_ge(ln_rstd, 4 * n)

            def layer_norm(src, dst, n, stats, between=None, meanwhile=None, before_out=None):
                c = ln_part(n)
                for h in range(2):
                    if h == 1 and between is not None:
                        between()
                    nc.vector.bn_stats(c["bn"][:, 6 * h:6 * h + 6], blk(src, h)).then_inc(ln_bn, 1)
                dve.wait_ge(ln_bn, 2 * stats)
                nc.vector.bn_aggr(c["ag"], c["bn"]).then_inc(ln_ag, 1)
                dve.wait_ge(ln_ag, stats)
                nc.vector.tensor_scalar(c["ve"], c["ag"][:, 1:2], EPS, None, ALU.add).then_inc(ln_var, 1)
                if meanwhile is not None:
                    meanwhile()
                inverse_root(n)
                if before_out is not None:
                    before_out()
                nc.vector.tensor_scalar(dst, src, c["ag"][:, 0:1], c["rstd"], ALU.subtract,
                                        ALU.mult).then_inc(ln_out, 1)

            def rotate(m, b, again=True):
                dve.wait_ge(kproj, KB * m + b + 1)
                src, cs, sn = blk(pk, b), blk(cosk, b), blk(sink, b)
                nc.vector.tensor_tensor(blk(krot, b), src, cs, ALU.mult).then_inc(k_mul, 1)
                if again:
                    dve.wait_ge(k_rot, KB * m + b)
                nc.vector.tensor_tensor(kswap[0:64, :], src[64:128, :], sn[64:128, :], ALU.mult).then_inc(k_mul, 1)
                nc.vector.tensor_tensor(kswap[64:128, :], src[0:64, :], sn[0:64, :], ALU.mult).then_inc(k_mul, 1)
                dve.wait_ge(k_mul, 3 * (KB * m + b + 1))
                nc.vector.tensor_tensor(blk(krot, b), blk(krot, b), kswap[:, :], ALU.add).then_inc(k_rot, 1)

            def k_los(m):
                for b in range(KB):
                    lo(blk(k_lo, b), blk(krot, b), blk(k_hi, b), k_l, (k_h, KB * m + b + 1))

            def v_los(m):
                for b in range(KB):
                    lo(blk(v_lo, b), blk(pa, b), blk(v_hi, b), v_l, (v_h, KB * m + b + 1))

            def rotate_q(m):
                dve.wait_ge(qproj, m + 1)
                q = blk(ps, 1).rearrange("p (h two d) -> p h two d", h=G, two=2)
                cos = cosq[:, :].unsqueeze(1).broadcast_to([P, G, DK])
                sin = sinq[:, :].rearrange("p (two d) -> p two d", two=2).unsqueeze(1).broadcast_to([P, G, 2, DK // 2])
                prod = blk(soft, 2)
                swap = blk(soft, 3).rearrange("p (h two d) -> p h two d", h=G, two=2)
                nc.vector.tensor_tensor(prod.rearrange("p (h d) -> p h d", h=G),
                                        blk(ps, 1).rearrange("p (h d) -> p h d", h=G), cos, ALU.mult).then_inc(q_mul, 1)
                for i in range(2):
                    nc.vector.tensor_tensor(swap[:, :, i, :], q[:, :, 1 - i, :], sin[:, :, i, :],
                                            ALU.mult).then_inc(q_mul, 1)
                dve.wait_ge(q_mul, 3 * m + 3)
                nc.vector.tensor_tensor(prod, prod, blk(soft, 3), ALU.add).then_inc(q_rot, 1)

            def q_lo_0(m):
                lo(q_lo.rearrange("p (h t) -> p h t", h=G),
                   blk(ps, 0).rearrange("p (h b t) -> p b h t", h=G, b=B)[:, 0],
                   q_hi.rearrange("p (h t) -> p h t", h=G), q_l, (q_h, 2 * m + 2))

            def q_lo_1(m):
                lo(q_lo[:, :], q1[:, bass.ds((m - HKV) * (G * SQ), G * SQ)], q_hi[:, :], q_l, (q_h, 2 * m + 2))

            def softmax(s, batch):
                for i in range(4):
                    if i < 2:
                        dve.wait_ge(vtr, KB * s + i + 1)
                    elif i == 2 and batch == 0:
                        dve.wait_ge(qtr, s + 1)
                    dve.wait_ge(scored, 4 * s + i + 1)
                    nc.vector.memset(gate[:, i:i + 1], 0.0)
                    dve.wait_ge(mask_in, 32 * (batch + 1))
                    nc.vector.tensor_tensor_reduce(
                        out=blk(soft, i), in0=blk(ps, i % 2), in1=blk(maskt, i % 2), scale=1.0, scalar=LOWEST,
                        op0=ALU.add, op1=ALU.max, accum_out=mx[:, i:i + 1]).then_inc(masked, 1)
                    if i % 2:
                        t = i // 2
                        dve.wait_ge(masked, 4 * s + i + 1)
                        nc.vector.tensor_scalar(nm[:, t:t + 1], mx[:, i - 1:i], mx[:, i:i + 1], -1.0,
                                                ALU.max, ALU.mult).then_inc(nmax, 1)

            def divide(s):
                for t in range(2):
                    dve.wait_ge(expd, 2 * s + t + 1)
                    nc.vector.reciprocal(ri[:, t:t + 1], rs[:, t:t + 1]).then_inc(recip, 1)
                    dve.wait_ge(recip, 2 * s + t + 1)
                    nc.vector.tensor_scalar(blk(soft, t, SK), blk(soft, t, SK), ri[:, t:t + 1], None,
                                            ALU.mult).then_inc(prob, 1)

            def pt_los(s, turns):
                for i in turns:
                    lo(blk(pt_lo, i % 2), blk(pa, i % 2), blk(pt_hi, i % 2), pt_l, (pt_h, 4 * s + i + 1))

            ol, oh = (t.rearrange("p (h b t) -> p b h t", h=G, b=B) for t in (o_lo, o_hi))

            def o_lo_0(s):
                dve.wait_ge(o_h, 2 * (s - HKV) + 1)
                nc.vector.tensor_tensor(ol[:, 0], o0[:, bass.ds((s - HKV) * (G * SQ), G * SQ)]
                                        .rearrange("p (h t) -> p h t", h=G), oh[:, 0], ALU.subtract)

            def o_lo_1(s):
                lo(ol[:, 1], ps[:, 0:G * SQ].rearrange("p (h t) -> p h t", h=G), oh[:, 1], o_l,
                   (o_h, 2 * (s - HKV) + 2))

            nc.vector.memset(ones[:, :], 1.0).then_inc(ones_set, 1)
            for n, kind, j in PROLOGUE:
                unit(Unit(n), *{"wk": (wk_hi, wk_lo), "wv": (wv_hi, wv_lo), "ctx": (ctx_hi, ctx_lo)}[kind], j)
            dve.wait_ge(x_in, 32)
            layer_norm(soft[:, 0:D], soft[:, D:2 * D], 1, 1)
            for j in range(2):
                unit(Unit(FIRST_W + j), w_hi, w_lo, j)
            dve.wait_ge(tab_in, 32)
            rotate(0, 0, again=False)
            for n in range(2):
                lo(blk(xt_lo, n), blk(ps, n), blk(xt_hi, n), xt_l, (xt_h, n + 1))
            for j in range(2, W_U):
                unit(Unit(FIRST_W + j), w_hi, w_lo, j)
            rotate(0, 1)
            dve.wait_ge(qtab_in, 32)
            rotate_q(0)
            k_los(0)
            q_lo_0(0)
            for j in range(WK_U):
                unit(Unit(FIRST_WK1 + j), wk_hi, wk_lo, j)

            def step_dve(s, at, batch):
                step = Step(s, at)
                w_dst, w_at = ((ctx_hi, ctx_lo), CH) if at == HKV - 1 else ((w_hi, w_lo), 0)
                softmax(s, batch)
                v_los(s)
                divide(s)
                if at == STEPS - 1:
                    pt_los(s, (0, 1))
                    o_lo_0(s)
                    unit(step.w(0), w_hi, w_lo, 0)
                    pt_los(s, (2,))
                    unit(step.w(1), w_hi, w_lo, 1)
                    pt_los(s, (3,))
                    for j in range(2, 4):
                        unit(step.w(j), w_hi, w_lo, j)
                    o_lo_1(s)
                    for j in range(4, W_U):
                        unit(step.w(j), w_hi, w_lo, j)
                    return
                if batch == 1:
                    o_lo_0(s)
                for j in range(4):
                    unit(step.w(j), *w_dst, w_at + j)
                pt_los(s, (0, 1))
                for j in range(4, W_U):
                    unit(step.w(j), *w_dst, w_at + j)
                for j in range(WV_U):
                    unit(step.wv(j), wv_hi, wv_lo, j)
                pt_los(s, (2, 3))
                if batch == 1:
                    o_lo_1(s)
                for b in range(KB):
                    rotate(s + 1, b)
                k_los(s + 1)
                if at < STEPS - 2:
                    for j in range(WK_U):
                        unit(step.wk(j), wk_hi, wk_lo, j)
                if at < HKV - 1:
                    rotate_q(s + 1)
                    q_lo_0(s + 1)
                else:
                    q_lo_1(s + 1)
                if at == HKV - 2:
                    for j in range(CH):
                        unit(Unit(CTX1 + j), ctx_hi, ctx_lo, j)

            with dve.Fori(0, HKV - 2) as s:
                step_dve(s, 0, 0)
            step_dve(HKV - 2, HKV - 2, 0)
            step_dve(HKV - 1, HKV - 1, 0)
            with dve.Fori(HKV, STEPS - 2) as s:
                step_dve(s, HKV, 1)
            step_dve(STEPS - 2, STEPS - 2, 1)
            step_dve(STEPS - 1, STEPS - 1, 1)

            for j in range(CH // 2):
                unit(Unit(TAB_U + j), ctx_hi, ctx_lo, CH // 2 + j)

            def gates(n, during_exp=None):
                nc.vector.memset(lg, LOWEST).then_inc(lg_in, 1)
                dve.wait_ge(lg_in, 4 * n - 3)
                dve.wait_ge(lora, n)
                nc.vector.tensor_copy(lg[:, 0:E], pa[:, UW:UW + E]).then_inc(lg_in, 1)
                dve.wait_ge(lg_in, 4 * n - 2)
                nc.vector.max(top_e[:, :], lg).then_inc(top_out, 1)
                dve.wait_ge(top_out, n)
                nc.vector.tensor_scalar(top_neg, top_e[:, 0:1], -1.0, None, ALU.mult).then_inc(lg_top, 1)
                nc.vector.max_index(idx_e[:, :], top_e[:, :], lg).then_inc(g_step, 1)
                dve.wait_ge(g_step, 6 * n - 5)
                nc.vector.tensor_copy(idxf, idx_e[:, :]).then_inc(g_step, 1)
                dve.wait_ge(g_step, 6 * n - 4)
                dve.wait_ge(late_in, 48)
                nc.vector.tensor_scalar(sel[:, 0:E], iota4, idxf[:, 0:1], None, ALU.is_equal).then_inc(g_step, 1)
                dve.wait_ge(g_step, 6 * n - 3)
                nc.vector.scalar_tensor_tensor(out=sel[:, E:2 * E], in0=iota4, scalar=idxf[:, 1:2], in1=sel[:, 0:E],
                                               op0=ALU.is_equal, op1=ALU.add).then_inc(g_step, 1)
                if during_exp is not None:
                    during_exp()
                dve.wait_ge(g_step, 6 * n - 2)
                dve.wait_ge(g_exp, n)
                nc.vector.tensor_tensor_reduce(out=gs, in0=ex, in1=sel[:, E:2 * E], scale=1.0, scalar=0.0,
                                               op0=ALU.mult, op1=ALU.add, accum_out=gsum).then_inc(lg_in, 1)
                dve.wait_ge(lg_in, 4 * n - 1)
                nc.vector.reciprocal(grec, gsum).then_inc(lg_in, 1)
                dve.wait_ge(lg_in, 4 * n)
                nc.vector.tensor_scalar(gs, gs, grec, float(LORA_SCALE), ALU.mult, ALU.mult).then_inc(g_step, 1)
                dve.wait_ge(g_step, 6 * n - 1)
                nc.vector.tensor_tensor(kswap[:, 0:E * R].rearrange("p (e r) -> p e r", e=E),
                                        pa[:, UW + E:UW + E + E * R].rearrange("p (e r) -> p e r", e=E),
                                        gs.unsqueeze(2).broadcast_to([P, E, R]), ALU.mult).then_inc(g_step, 1)
                dve.wait_ge(mid_ps, n)
                nc.vector.tensor_copy(kswap[0:E * R, 128:256], pa[0:E * R, 0:P]).then_inc(mid_t, 1)

            def h_copy(n):
                dve.wait_ge(h_ps, 2 * n)
                nc.vector.tensor_copy(blk(maskt, 1), blk(ps, 1)).then_inc(h_t1, 1)

            def add_delta(n):
                dve.wait_ge(x2_done, 1)
                for h in range(2):
                    dve.wait_ge(delta, 2 * n + h - 1)
                    nc.vector.tensor_tensor(blk(soft, h), blk(soft, h), blk(pk, h), ALU.add).then_inc(y_out, 1)

            xn = q1[:, 0:D]

            def fold_odd():
                dve.wait_ge(x1_copy, 1)
                nc.vector.tensor_tensor(blk(q1, 3), blk(py, 0), blk(q1, 3), ALU.subtract).then_inc(fold, 1)

            first, second = ln_part(2), ln_part(3)

            def variance_2():
                nc.vector.tensor_scalar(grown, first["rstd"], 1.0, None, ALU.add).then_inc(x2_stat, 1)
                dve.wait_ge(x2_stat, 1)
                nc.vector.scalar_tensor_tensor(out=second["ve"], in0=grown, scalar=grown, in1=first["ag"][:, 1:2],
                                               op0=ALU.mult, op1=ALU.mult).then_inc(x2_stat, 1)
                dve.wait_ge(x2_stat, 2)
                nc.vector.tensor_scalar(second["ve"], second["ve"], EPS, None, ALU.add).then_inc(ln_var, 1)

            def odd_lo():
                lo(blk(xt_lo, 1), blk(pk, 1), blk(xt_hi, 1), ab_l, (ab_h, 1))

            dve.wait_ge(w_used, HKV)
            layer_norm(py[:, :], xn, 2, 2, fold_odd, odd_lo, variance_2)
            dve.wait_ge(ln_out, 2)
            nc.vector.tensor_tensor(blk(q1, 2), blk(xn, 0), blk(xn, 1), ALU.add).then_inc(fold, 1)
            inverse_root(3)
            nc.vector.tensor_tensor(grown, grown, second["rstd"], ALU.mult).then_inc(x2_stat, 1)
            dve.wait_ge(x2_stat, 3)
            nc.vector.tensor_scalar(soft[:, D:2 * D], py[:, :], first["ag"][:, 0:1], grown, ALU.subtract,
                                    ALU.mult).then_inc(ln_out, 1)
            lo(blk(xt_lo, 0), blk(pk, 0), blk(xt_hi, 0), ab_l, (ab_h, 2))
            x2 = soft[:, 0:D]

            def inverse_unit(j):
                unit(Unit(INV_U + j), ctx_hi, ctx_lo, j, first=F_COLS, cols=2 * LAGS)

            inverse_unit(0)
            h_copy(1)
            inverse_unit(1)
            lo(blk(k_lo, 1), blk(pk, 1), blk(k_hi, 1), sq_l, (sq_h, 1))
            for j in range(2, CH // 2):
                inverse_unit(j)
            nc.vector.tensor_tensor(x2, py[:, :], xn, ALU.add).then_inc(x2_done, 1)

            L0 = HALF // 2 + 1
            corr = o0[:, D:D + HALF + 1]

            gates(1, lambda: lo(blk(k_lo, 0), blk(pk, 0), blk(k_hi, 0), sq_l, (sq_h, 2)))
            dve.wait_ge(even_out, 1)
            dve.wait_ge(idft, 2)
            nc.vector.tensor_tensor(corr[:, 0:L0], krot[:, 0:L0], ps[:, UW:UW + L0], ALU.add).then_inc(lagged, 1)
            nc.vector.tensor_tensor(corr[:, L0:HALF + 1], krot[:, 0:L0 - 1], ps[:, UW:UW + L0 - 1],
                                    ALU.subtract).then_inc(lagged, 1)
            dve.wait_ge(lagged, 2)
            nc.vector.max(top8[:, :], corr).then_inc(topped, 1)
            add_delta(1)
            dve.wait_ge(topped, 1)
            nc.vector.tensor_scalar(neg0, top8[:, 0:1], -1.0, None, ALU.mult).then_inc(gapped, 1)
            nc.vector.tensor_scalar(gap, top8[:, 1:2], top8[:, 0:1], None, ALU.subtract).then_inc(gapped, 1)
            dve.wait_ge(gapped, 2)
            nc.vector.tensor_scalar(near, gap, -110.0, None, ALU.is_ge).then_inc(gapped, 1)
            dve.wait_ge(near_ps, 1)
            nc.vector.tensor_copy(flag_i[0:1, 0:1], ps[0:1, UW - 1:UW]).then_inc(flagged, 1)
            dve.wait_ge(flagged, 1)
            rows_near = dve.value_load(flag_i[0:1, 0:1], min_val=0, max_val=P)
            with dve.If(rows_near > 0):
                dve.wait_ge(weighed, 1)
                dve.wait_ge(out_done, 32)
                delayed_sum(nc, dve, gen, st, e8, top8, idx8, corr, q1, py, x2)
                layer_norm(x2, soft[:, D:2 * D], 4, 3)
                h_copy(2)
                gates(2)
                add_delta(2)


def delayed_sum(nc, dve, gen, st, e8, top8, idx8, corr, q1, py, x2):
    count = [0]

    def done(ins):
        count[0] += 1
        ins.then_inc(gen, 1)
        dve.wait_ge(gen, count[0])

    V = nc.vector
    lag, mult, taken, weight = st[:, 66:74], st[:, 74:82], st[:, 82:90], st[:, 28:36]
    lags, weights = st[:, 36:52], st[:, 52:60]
    tmp, tau, coef, total = st[:, 90:91], st[:, 91:92], st[:, 92:93], st[:, 93:94]
    n0 = float(HALF // 2 + 1)
    done(V.max_index(idx8[:, :], top8[:, :], corr))
    done(V.tensor_copy(lag, idx8[:, :]))
    done(V.tensor_scalar(mult, lag, n0, None, ALU.is_ge))
    done(V.tensor_scalar(taken, lag, -2.0, float(3 * HALF // 2 + 1), ALU.mult, ALU.add))
    done(V.tensor_tensor(taken, taken, mult, ALU.mult))
    done(V.tensor_tensor(lag, lag, taken, ALU.add))
    done(V.tensor_scalar(mult, lag, 0.0, -1.0, ALU.is_equal, ALU.mult))
    done(V.tensor_scalar(taken, lag, float(HALF), None, ALU.is_equal))
    done(V.tensor_tensor(mult, mult, taken, ALU.subtract))
    done(V.tensor_scalar(mult, mult, 2.0, None, ALU.add))
    done(V.memset(taken[:, 0:1], float(TOPK)))
    for j in range(1, 8):
        done(V.tensor_tensor(taken[:, j:j + 1], taken[:, j - 1:j], mult[:, j - 1:j], ALU.subtract))
    done(V.tensor_scalar(taken, taken, 0.0, None, ALU.max))
    done(V.tensor_tensor(taken, taken, mult, ALU.min))
    done(V.tensor_copy(weight, e8))
    done(V.tensor_tensor(weights, weight, taken, ALU.mult))
    done(V.tensor_reduce(total, weights, mybir.AxisListType.X, ALU.add))
    done(V.reciprocal(tmp, total))
    done(V.tensor_scalar(weight, weight, tmp, None, ALU.mult))
    done(V.tensor_copy(lags[:, 0:8], lag))
    done(V.tensor_scalar(lags[:, 8:16], lag, -1.0, float(D), ALU.mult, ALU.add))
    done(V.scalar_tensor_tensor(out=mult, in0=taken, scalar=2.0, in1=weight, op0=ALU.is_ge, op1=ALU.mult))
    done(V.scalar_tensor_tensor(out=weight, in0=taken, scalar=1.0, in1=weight, op0=ALU.is_ge, op1=ALU.mult))
    done(V.tensor_copy(q1[:, D:2 * D], q1[:, 0:D]))
    done(V.tensor_copy(x2, py[:, :]))
    done(V.memset(tau, 0.0))
    with dve.Fori(0, D) as t:
        n = count[0] + 6 * t
        steps = (
            lambda: V.scalar_tensor_tensor(out=taken, in0=lags[:, 0:8], scalar=tau, in1=weight, op0=ALU.is_equal,
                                           op1=ALU.mult),
            lambda: V.scalar_tensor_tensor(out=weights, in0=lags[:, 8:16], scalar=tau, in1=mult, op0=ALU.is_equal,
                                           op1=ALU.mult),
            lambda: V.tensor_tensor(taken, taken, weights, ALU.add),
            lambda: V.tensor_reduce(coef, taken, mybir.AxisListType.X, ALU.add),
            lambda: V.scalar_tensor_tensor(out=x2, in0=q1[:, bass.ds(t, D)], scalar=coef, in1=x2, op0=ALU.mult,
                                           op1=ALU.add),
            lambda: V.tensor_scalar(tau, tau, 1.0, None, ALU.add),
        )
        for i, step in enumerate(steps):
            step().then_inc(gen, 1)
            dve.wait_ge(gen, n + i + 1)


def tables():
    f32 = np.float32
    half = np.arange(0, DK, 2, dtype=f32) / f32(DK)
    inv = (f32(1.0) / np.power(f32(10000.0), half)).astype(f32)
    ang = np.arange(SK, dtype=f32)[:, None] * inv[None, :]
    cos, sin = np.cos(ang.astype(np.float64)), np.sin(ang.astype(np.float64))
    cos_k = np.concatenate([cos, cos], 1).T.astype(f32)
    sin_k = np.concatenate([sin, -sin], 1).T.astype(f32)
    scale = 1.0 / np.sqrt(float(DK))
    cos_q = np.tile(np.concatenate([cos, cos], 1)[:SQ] * scale, (B, 1)).astype(f32)
    sin_q = np.tile(np.concatenate([-sin, sin], 1)[:SQ] * scale, (B, 1)).astype(f32)
    t = np.arange(HALF)[:, None]

    def angle(f, u):
        return 2 * np.pi * ((f * u) % D) / D

    fe_re, fe_im = np.arange(0, HALF + 1, 2), np.arange(2, HALF, 2)
    fo = np.arange(1, HALF, 2)
    fwd_e = np.concatenate([np.cos(angle(fe_re[None], t)), -np.sin(angle(fe_im[None], t))], 1)
    fwd_o = np.concatenate([np.cos(angle(fo[None], t)), -np.sin(angle(fo[None], t))], 1)
    lag = np.arange(LAGS)[None, :]
    wt = np.where((fe_re == 0) | (fe_re == HALF), 1.0, 2.0)[:, None]
    inv_e = np.concatenate([wt * np.cos(angle(fe_re[:, None], lag)), 2 * np.cos(angle(fe_im[:, None], lag))], 0) / D
    one = 2 * np.cos(angle(fo[:, None], lag)) / D
    one[:, HALF // 2] = 0.0
    inv_o = np.concatenate([one, one], 0)

    tab_e = fwd_e.astype(f32)
    tab_e_hi = (tab_e.view(np.int32) & np.int32(-1 << 12)).view(f32)
    tab_e = np.stack([tab_e_hi, tab_e - tab_e_hi]).reshape(2, 4, P, UW).transpose(0, 2, 1, 3).reshape(2, P, 4 * UW)
    tab_o = fwd_o.reshape(4, P, UW).astype(f32)
    tab_i = np.concatenate([inv_e, inv_o], 0).astype(f32)
    tab_i = tab_i.reshape(CH // 2, 2, P, LAGS).transpose(0, 2, 1, 3).reshape(CH // 2, P, 2 * LAGS)
    return dict(tab_e=tab_e, tab_o=tab_o, tab_i=tab_i, cos_k=cos_k, sin_k=sin_k, cos_q=cos_q, sin_q=sin_q,
                ident=np.eye(P, dtype=f32), iota=np.tile(np.arange(E, dtype=f32), (P, 1)))


def kernel(x, ctx_4096, mask_BxSxS2_ff0, L0_xattn_wq, L0_xattn_wk, L0_xattn_wv, L0_xattn_wo, L0_ffn_A, L0_ffn_B,
           L0_ffn_Wr):
    import concourse.bacc as bacc
    from concourse.bass_utils import run_bass_kernel_spmd

    def wkv_units(w):
        return w.reshape(2, 4, P, HKV, DK).transpose(3, 0, 2, 1, 4).reshape(HKV, 2, P, UW)

    c = tables()
    arrays = {
        "x": x.reshape(T, D),
        "ctx_u": ctx_4096.reshape(B, KB, UW, CH, P).transpose(0, 1, 3, 4, 2).reshape(B, CTX_U, P, UW),
        "mask": mask_BxSxS2_ff0,
        "wkv_u": np.concatenate([wkv_units(np.asarray(L0_xattn_wk)), wkv_units(np.asarray(L0_xattn_wv))], 1),
        "wq_u": np.asarray(L0_xattn_wq).reshape(CH, P, HKV, UW).transpose(2, 0, 1, 3),
        "wo_u": np.asarray(L0_xattn_wo).reshape(HKV, G, P, 2, UW).transpose(0, 1, 3, 2, 4).reshape(HKV, W_U, P, UW),
        "tab_e": c["tab_e"], "tab_o": c["tab_o"], "tab_i": c["tab_i"], "cos_k": c["cos_k"], "sin_k": c["sin_k"],
        "cos_q": c["cos_q"], "sin_q": c["sin_q"], "ident_d": c["ident"],
        "aw": np.concatenate([np.asarray(L0_ffn_Wr).T, np.asarray(L0_ffn_A).reshape(E * R, D).T], 1)
        .reshape(CH, P, E + E * R).transpose(1, 0, 2).reshape(P, CH * (E + E * R)),
        "bt": np.asarray(L0_ffn_B).transpose(0, 2, 1).reshape(E * R, D),
        "iota_d": c["iota"],
    }
    arrays = {k: np.ascontiguousarray(v) for k, v in arrays.items()}
    nc = bacc.Bacc("TRN2", target_bir_lowering=False, num_devices=1)
    args = {k: nc.dram_tensor(k + "_dram", list(v.shape), mybir.dt.from_np(v.dtype), kind="ExternalInput").ap()
            for k, v in arrays.items()}
    out = nc.dram_tensor("out_dram", [T, D], F32, kind="ExternalOutput").ap()
    perceiver_kernel(nc, out=out, **args)
    r = run_bass_kernel_spmd(nc, [{k + "_dram": v for k, v in arrays.items()}], core_ids=[0])
    return r.results[0]["out_dram"].reshape(B, SQ, D)
```
